# Optimizing a Trainium2 kernel written in Bass

```python
import numpy as np
import jax
import jax.numpy as jnp

def _softmax(x, axis=-1):
    return jax.nn.softmax(x, axis=axis)

def _gelu(x):
    return jax.nn.gelu(x, approximate=True)

def _silu(x):
    return jax.nn.silu(x)

def _sigmoid(x):
    return jax.nn.sigmoid(x)

def _layernorm(x, axis=-1, eps=1e-05):
    m = jnp.mean(x, axis=axis, keepdims=True)
    v = jnp.var(x, axis=axis, keepdims=True)
    return (x - m) / jnp.sqrt(v + eps)

def _scatter_add(tgt, idx, src, axis=0):
    return tgt.at[idx].add(src)

def _segment_sum(src, seg, n):
    return jax.ops.segment_sum(src, seg, n)
kernel_name = 'mk_sandwich_d1_jaxref_r8_544a1e'

def setup_inputs(seed: int=0):
    np.random.seed(seed)
    _w = jnp.asarray

    def _L0_attn_setup():
        import jax, jax.numpy as jnp
        import numpy as np
        B, S, HID = (1, 256, 128)
        H, HKV, D = (16, 4, 64)
        THETA = 10000.0

        def _rope_tables(seq_len, head_dim):
            inv_freq = 1.0 / THETA ** (jnp.arange(0, head_dim, 2, dtype=jnp.float32) / head_dim)
            freqs = jnp.arange(seq_len, dtype=jnp.float32)[:, None] * inv_freq[None, :]
            emb = jnp.concatenate([freqs, freqs], axis=-1)
            return (jnp.cos(emb)[:, 0::2], jnp.sin(emb)[:, 0::2])

        def _apply_rope(x, cos, sin):
            xe, xo = (x[..., 0::2], x[..., 1::2])
            re = xe * cos - xo * sin
            ro = xe * sin + xo * cos
            return jnp.stack([re, ro], axis=-1).reshape(x.shape)
        key = jax.random.key(seed)
        k0, k1, k2, k3, k4 = jax.random.split(key, 5)
        return {'hidden_states': jax.random.normal(k0, (B, S, HID), dtype=jnp.float32), 'Wq': jax.random.normal(k1, (HID, H * D), dtype=jnp.float32) * 0.02, 'Wk': jax.random.normal(k2, (HID, HKV * D), dtype=jnp.float32) * 0.02, 'Wv': jax.random.normal(k3, (HID, HKV * D), dtype=jnp.float32) * 0.02, 'Wo': jax.random.normal(k4, (H * D, HID), dtype=jnp.float32) * 0.02}
    _L0_attn_in = _L0_attn_setup()

    def _L0_ffn_setup():
        import jax, jax.numpy as jnp
        import numpy as np
        B, S, D = (2, 256, 128)
        E, K, H = (8, 4, 128)
        SH = 2 * H

        def _silu(x):
            return x * jax.nn.sigmoid(x)

        def _swiglu(x, w1, b1, w2, b2):
            return _silu(x @ w1 + b1) * (x @ w2 + b2)

        def _moe(x, gate_w, exp_w1, exp_w3, exp_w2, sh_w1, sh_w3, sh_w2):
            b, s, d = x.shape
            t = b * s
            xt = x.reshape(t, d)
            scores = jax.nn.softmax(xt @ gate_w.T, axis=-1)
            topv, topi = jax.lax.top_k(scores, K)
            topv = topv / jnp.sum(topv, axis=-1, keepdims=True)
            combine = jnp.zeros((t, E), xt.dtype).at[jnp.arange(t)[:, None], topi].set(topv)
            g = _silu(jnp.einsum('td,edh->eth', xt, exp_w1))
            u = jnp.einsum('td,edh->eth', xt, exp_w3)
            yexp = jnp.einsum('eth,ehd->etd', g * u, exp_w2)
            routed = jnp.einsum('te,etd->td', combine, yexp)
            shared = _silu(xt @ sh_w1) * (xt @ sh_w3) @ sh_w2
            return (routed + shared).reshape(b, s, d)
        key = jax.random.key(seed)
        ks = jax.random.split(key, 24)
        f = lambda k, shape: jax.random.normal(k, shape, dtype=jnp.float32) * 0.02
        return {'x': jax.random.normal(ks[0], (B, S, D), dtype=jnp.float32), 'lin0_w': f(ks[1], (D, D)), 'lin0_b': f(ks[2], (D,)), 'swi1_w1': f(ks[3], (D, D)), 'swi1_b1': f(ks[4], (D,)), 'swi1_w2': f(ks[5], (D, D)), 'swi1_b2': f(ks[6], (D,)), 'gate_w': f(ks[7], (E, D)), 'exp_w1': f(ks[8], (E, D, H)), 'exp_w3': f(ks[9], (E, D, H)), 'exp_w2': f(ks[10], (E, H, D)), 'sh_w1': f(ks[11], (D, SH)), 'sh_w3': f(ks[12], (D, SH)), 'sh_w2': f(ks[13], (SH, D)), 'lin1_w': f(ks[14], (D, D)), 'lin1_b': f(ks[15], (D,)), 'swi2_w1': f(ks[16], (D, D)), 'swi2_b1': f(ks[17], (D,)), 'swi2_w2': f(ks[18], (D, D)), 'swi2_b2': f(ks[19], (D,))}
    _L0_ffn_in = _L0_ffn_setup()
    _d = {'L0_attn_hidden_states': _L0_attn_in['hidden_states'], 'L0_attn_Wq': _L0_attn_in['Wq'], 'L0_attn_Wk': _L0_attn_in['Wk'], 'L0_attn_Wv': _L0_attn_in['Wv'], 'L0_attn_Wo': _L0_attn_in['Wo'], 'L0_ffn_lin0_w': _L0_ffn_in['lin0_w'], 'L0_ffn_lin0_b': _L0_ffn_in['lin0_b'], 'L0_ffn_swi1_w1': _L0_ffn_in['swi1_w1'], 'L0_ffn_swi1_b1': _L0_ffn_in['swi1_b1'], 'L0_ffn_swi1_w2': _L0_ffn_in['swi1_w2'], 'L0_ffn_swi1_b2': _L0_ffn_in['swi1_b2'], 'L0_ffn_gate_w': _L0_ffn_in['gate_w'], 'L0_ffn_exp_w1': _L0_ffn_in['exp_w1'], 'L0_ffn_exp_w3': _L0_ffn_in['exp_w3'], 'L0_ffn_exp_w2': _L0_ffn_in['exp_w2'], 'L0_ffn_sh_w1': _L0_ffn_in['sh_w1'], 'L0_ffn_sh_w3': _L0_ffn_in['sh_w3'], 'L0_ffn_sh_w2': _L0_ffn_in['sh_w2'], 'L0_ffn_lin1_w': _L0_ffn_in['lin1_w'], 'L0_ffn_lin1_b': _L0_ffn_in['lin1_b'], 'L0_ffn_swi2_w1': _L0_ffn_in['swi2_w1'], 'L0_ffn_swi2_b1': _L0_ffn_in['swi2_b1'], 'L0_ffn_swi2_w2': _L0_ffn_in['swi2_w2'], 'L0_ffn_swi2_b2': _L0_ffn_in['swi2_b2']}
    _x0 = _d['L0_attn_hidden_states']
    _d['L0_attn_hidden_states'] = jax.random.normal(jax.random.fold_in(jax.random.key(seed), 1), (4, 1024, 128), dtype=_x0.dtype)
    del _x0
    return _d

def reference(L0_attn_hidden_states, L0_attn_Wq, L0_attn_Wk, L0_attn_Wv, L0_attn_Wo, L0_ffn_lin0_w, L0_ffn_lin0_b, L0_ffn_swi1_w1, L0_ffn_swi1_b1, L0_ffn_swi1_w2, L0_ffn_swi1_b2, L0_ffn_gate_w, L0_ffn_exp_w1, L0_ffn_exp_w3, L0_ffn_exp_w2, L0_ffn_sh_w1, L0_ffn_sh_w3, L0_ffn_sh_w2, L0_ffn_lin1_w, L0_ffn_lin1_b, L0_ffn_swi2_w1, L0_ffn_swi2_b1, L0_ffn_swi2_w2, L0_ffn_swi2_b2):

    def _L0_attn_ref(hidden_states, Wq, Wk, Wv, Wo):
        import jax, jax.numpy as jnp
        import numpy as np
        B, S, HID = (1, 256, 128)
        H, HKV, D = (16, 4, 64)
        THETA = 10000.0

        def _rope_tables(seq_len, head_dim):
            inv_freq = 1.0 / THETA ** (jnp.arange(0, head_dim, 2, dtype=jnp.float32) / head_dim)
            freqs = jnp.arange(seq_len, dtype=jnp.float32)[:, None] * inv_freq[None, :]
            emb = jnp.concatenate([freqs, freqs], axis=-1)
            return (jnp.cos(emb)[:, 0::2], jnp.sin(emb)[:, 0::2])

        def _apply_rope(x, cos, sin):
            xe, xo = (x[..., 0::2], x[..., 1::2])
            re = xe * cos - xo * sin
            ro = xe * sin + xo * cos
            return jnp.stack([re, ro], axis=-1).reshape(x.shape)
        b, s, _ = hidden_states.shape
        q = (hidden_states @ Wq).reshape(b, s, H, D).transpose(0, 2, 1, 3)
        k = (hidden_states @ Wk).reshape(b, s, HKV, D).transpose(0, 2, 1, 3)
        v = (hidden_states @ Wv).reshape(b, s, HKV, D).transpose(0, 2, 1, 3)
        cos, sin = _rope_tables(s, D)
        q = _apply_rope(q, cos, sin)
        k = _apply_rope(k, cos, sin)
        G = H // HKV
        qg = q.reshape(b, HKV, G, s, D)
        scale = jnp.float32(D) ** (-0.5)
        scores = jnp.einsum('bkgqd,bkpd->bkgqp', qg, k) * scale
        causal = jnp.tril(jnp.ones((s, s), dtype=bool))
        scores = jnp.where(causal, scores, jnp.float32(-1e+30))
        probs = jax.nn.softmax(scores, axis=-1)
        out = jnp.einsum('bkgqp,bkpd->bkgqd', probs, v).reshape(b, H, s, D)
        out = out.transpose(0, 2, 1, 3).reshape(b, s, H * D)
        return out @ Wo

    def _L0_ffn_ref(x, lin0_w, lin0_b, swi1_w1, swi1_b1, swi1_w2, swi1_b2, gate_w, exp_w1, exp_w3, exp_w2, sh_w1, sh_w3, sh_w2, lin1_w, lin1_b, swi2_w1, swi2_b1, swi2_w2, swi2_b2):
        import jax, jax.numpy as jnp
        import numpy as np
        B, S, D = (2, 256, 128)
        E, K, H = (8, 4, 128)
        SH = 2 * H

        def _silu(x):
            return x * jax.nn.sigmoid(x)

        def _swiglu(x, w1, b1, w2, b2):
            return _silu(x @ w1 + b1) * (x @ w2 + b2)

        def _moe(x, gate_w, exp_w1, exp_w3, exp_w2, sh_w1, sh_w3, sh_w2):
            b, s, d = x.shape
            t = b * s
            xt = x.reshape(t, d)
            scores = jax.nn.softmax(xt @ gate_w.T, axis=-1)
            topv, topi = jax.lax.top_k(scores, K)
            topv = topv / jnp.sum(topv, axis=-1, keepdims=True)
            combine = jnp.zeros((t, E), xt.dtype).at[jnp.arange(t)[:, None], topi].set(topv)
            g = _silu(jnp.einsum('td,edh->eth', xt, exp_w1))
            u = jnp.einsum('td,edh->eth', xt, exp_w3)
            yexp = jnp.einsum('eth,ehd->etd', g * u, exp_w2)
            routed = jnp.einsum('te,etd->td', combine, yexp)
            shared = _silu(xt @ sh_w1) * (xt @ sh_w3) @ sh_w2
            return (routed + shared).reshape(b, s, d)
        h = x @ lin0_w + lin0_b
        h = _swiglu(h, swi1_w1, swi1_b1, swi1_w2, swi1_b2)
        h = _moe(h, gate_w, exp_w1, exp_w3, exp_w2, sh_w1, sh_w3, sh_w2)
        h = h @ lin1_w + lin1_b
        h = _swiglu(h, swi2_w1, swi2_b1, swi2_w2, swi2_b2)
        return h
    x = L0_attn_hidden_states
    x = x + _layernorm(_L0_attn_ref(_layernorm(x, axis=-1), L0_attn_Wq, L0_attn_Wk, L0_attn_Wv, L0_attn_Wo), axis=-1)
    x = x + _layernorm(_L0_ffn_ref(_layernorm(x, axis=-1), L0_ffn_lin0_w, L0_ffn_lin0_b, L0_ffn_swi1_w1, L0_ffn_swi1_b1, L0_ffn_swi1_w2, L0_ffn_swi1_b2, L0_ffn_gate_w, L0_ffn_exp_w1, L0_ffn_exp_w3, L0_ffn_exp_w2, L0_ffn_sh_w1, L0_ffn_sh_w3, L0_ffn_sh_w2, L0_ffn_lin1_w, L0_ffn_lin1_b, L0_ffn_swi2_w1, L0_ffn_swi2_b1, L0_ffn_swi2_w2, L0_ffn_swi2_b2), axis=-1)
    return x

_drawn_inputs = setup_inputs


def setup_inputs(seed=0):
    import zlib

    import numpy as np

    out = dict(_drawn_inputs(seed))
    spreads = {}
    factors = {'L0_ffn_lin0_w': 8.0,
     'L0_ffn_lin0_b': 8.0,
     'L0_ffn_swi1_w1': 8.0,
     'L0_ffn_swi1_b1': 8.0,
     'L0_ffn_swi1_w2': 8.0,
     'L0_ffn_swi1_b2': 8.0,
     'L0_ffn_gate_w': 8.0,
     'L0_ffn_exp_w1': 8.0,
     'L0_ffn_exp_w3': 8.0,
     'L0_ffn_exp_w2': 8.0,
     'L0_ffn_sh_w1': 8.0,
     'L0_ffn_sh_w3': 8.0,
     'L0_ffn_sh_w2': 8.0,
     'L0_ffn_lin1_w': 8.0,
     'L0_ffn_lin1_b': 3.718,
     'L0_ffn_swi2_w1': 5.545,
     'L0_ffn_swi2_w2': 5.259}
    for name, (base, spread) in spreads.items():
        noise = np.random.default_rng([zlib.crc32(name.encode()), seed]).standard_normal(out[name].shape)
        drawn = base * np.exp(spread * noise) if base else spread * noise
        out[name] = jnp.asarray(drawn.astype(out[name].dtype))
    for name, factor in factors.items():
        out[name] = (out[name] * factor).astype(out[name].dtype)
    return out
```

```python
from contextlib import ExitStack

import numpy as np
import concourse.bass as bass
from concourse import mybir

F32 = mybir.dt.float32
F32R = mybir.dt.float32r
BF16 = mybir.dt.bfloat16
ALU = mybir.AluOpType
ACT = mybir.ActivationFunctionType
AX_X = mybir.AxisListType.X

B, S, HID = 4, 1024, 128
HKV, D = 4, 64
PAIRS = 2
NP = HKV * PAIRS
TILES = S // 128
HALF = 512
UNITS = 2 * NP
NE, TOPK = 8, 4
FFN_STEPS = NE + 2
EPS = 1e-5
MASKED = -1e30
ROPE_THETA = 10000.0

E_RING, P_RING, M_RING = 3, 6, 2
LAG = 2

PROJ_A, PROJ_B = 4, 2
ROPES_G = PROJ_A + PROJ_B
ROPES_B = ROPES_G * HKV
PROBS_U = (8, 16)
PROBS_P = sum(PROBS_U)
PROBS_G = PAIRS * PROBS_P
PROBS_B = HKV * PROBS_G
SCORES_G = ROPES_G + PROBS_G
SCORES_B = HKV * SCORES_G
assert SCORES_G % E_RING == 0 and PROBS_P % P_RING == 0 and PROBS_P % M_RING == 0

C_ID, C_ONES, C_TIE, C_COS, C_SIN, C_EPS, C_F32 = 0, 128, 192, 256, 256 + S, 256 + 2 * S, 257 + 2 * S
FFN_LOADS = 20

NORMS = 6
SWAP = [i ^ 1 for i in range(32)]
STEPS_B = 2 + 2 * 3 + 2 + 2 * 1 + 1 + 2 * 12 + 2 * 3
C_IDB, C_TRIQ, C_TRIK, C_SEL, C_BF = 0, 128, 256, 384, 384 + NE * 128


def rope_index(b, g, k):
    return b * ROPES_B + g * ROPES_G + k


def score_index(b, g, where, k, last=False):
    ahead = 0 if last else PROJ_A
    first = {0: 0, "A": PROBS_P, 1: PROBS_P + ahead, "B": 2 * PROBS_P + PROJ_A}[where]
    return b * SCORES_B + ROPES_G + g * SCORES_G + first + k


def project_index(b, g, k):
    if isinstance(g, int) and g == 0:
        return b * SCORES_B + k
    return score_index(b, g - 1, "A", k) if k < PROJ_A else score_index(b, g - 1, "B", k - PROJ_A)


def pieces(c):
    out = []
    for h in range(2):
        for i in range(4 * c, 4 * c + 4):
            for kh in range(c + 1):
                out.append((h, i, kh, HALF if kh < c else (i - 4 * c + 1) * 128))
    if c:
        out = [x for h in range(2) for kh in range(2) for x in out if x[0] == h and x[2] == kh]
    return out


EARLY = 4


def piece_plan(c):
    if c == 1:
        plan = [[] for _ in range(8)]
        for n in range(8):
            plan[3 + n // 3 if n < 6 else 5].append((1, 0, n))
        for n in range(EARLY):
            plan[6 + n // 2].append((1, 1, n))
        return plan
    plan = [[] for _ in range(4)]
    for n in range(EARLY, 16):
        plan[(n - EARLY) // 4].append((0, 1, n))
    return plan


def prob_index(b, g, p, c, n):
    return b * PROBS_B + g * PROBS_G + p * PROBS_P + c * PROBS_U[0] + n


def unit_index(b, g, p, c):
    return b * UNITS + g * 4 + p * 2 + c


ROPE_PLAN = {
    (0, 0, 0): [("turn", 4)], (0, 0, 1): [("turn", 5), ("sum", 4)],
    (0, 0, 2): [("sum", 5), ("low", 4)], (0, 0, 3): [("low", 5)],
    (1, 0, 0): [("turn", 0)], (1, 0, 1): [("turn", 1), ("sum", 0)],
    (1, 0, 2): [("sum", 1), ("low", 0)], (1, 0, 3): [("low", 1), ("turn", 2)],
    (1, 1, 0): [("turn", 3), ("sum", 2)], (1, 1, 1): [("sum", 3), ("low", 2)], (1, 1, 2): [("low", 3)],
}


def build(nc, io, out):
    with ExitStack() as ctx:
        def sb(name, shape, dt=F32):
            return ctx.enter_context(nc.sbuf_tensor(name, shape, dt))

        def bank(name):
            return ctx.enter_context(nc.psum_tensor(name, [128, HALF], F32))

        def sem(name):
            return ctx.enter_context(nc.semaphore(name))

        cf = sb("cf", [128, C_F32])
        cb = sb("cb", [128, C_BF], BF16)
        ident, identb = cf[:, C_ID:C_ID + 128], cb[:, C_IDB:C_IDB + 128]
        ones = cf[:, C_ONES:C_ONES + D]
        tri_q, tri_k = cb[:, C_TRIQ:C_TRIQ + 128], cb[:, C_TRIK:C_TRIK + 128]
        biases = sb("biases", [128, 6])
        gate_wT = sb("gate_wT", [128, NE])
        w_lin0, w_lin1 = sb("w_lin0", [128, 128]), sb("w_lin1", [128, 128])
        w_swi = sb("w_swi", [128, 4, 128])
        w_exp = sb("w_exp", [128, 3, FFN_STEPS, 128])
        w_o = sb("w_o", [128, NP, HID])
        w_qk = sb("w_qk", [128, 2, HKV, 384], F32R)
        w_v = sb("w_v", [128, 2, HKV * D], F32R)
        slab_a = sb("slab_a", [128, 2, 256], F32R)
        slab_b = sb("slab_b", [128, 2, 128], F32R)
        x_in = sb("x_in", [128, TILES, HID])
        x_mid = sb("x_mid", [128, TILES, HID])
        stats = sb("stats", [128, TILES, 6])
        mean_var = sb("mean_var", [128, TILES, 2])
        dev = sb("dev", [128, TILES])
        rstd = sb("rstd", [128, TILES])
        unused = sb("unused", [128, 1])
        xT = sb("xT", [128, 2, S], F32R)
        v_all = sb("v_all", [128, TILES, HKV * D])
        v_g = [sb(f"v_g{p}", [128, TILES, D]) for p in range(2)]
        kk = [sb(f"kk{p}", [128, S], F32R) for p in range(2)]
        kl = [[sb(f"kl{p}{h}", [128, S], F32R) for h in range(2)] for p in range(2)]
        qa = [[sb(f"qa{p}{h}", [128, S], F32R) for h in range(2)] for p in range(2)]
        qb = [[sb(f"qb{p}{h}", [128, S], F32R) for h in range(2)] for p in range(2)]
        raw = sb("raw", [128, 4, HALF])
        turned = sb("turned", [128, 2, HALF])
        roped = sb("roped", [128, 2, HALF])
        probs = sb("probs", [128, P_RING, HALF])
        psums = sb("psums", [128, 2, 2, HALF])
        recip = sb("recip", [128, HALF])
        maxes = sb("maxes", [128, 2, 2, 2, 4])
        top = sb("top", [128, 2, 4])
        neg_max = sb("neg_max", [128, 2, 2, 4, 2], BF16)
        attnT = sb("attnT", [128, NP, S])
        def ffn_buf(n):
            return attnT[:, n, :].rearrange("p (c t) -> p c t", c=2)
        hT, aT, h1T, gT, guT, gucT, yT = (ffn_buf(n) for n in range(7))
        w_raw = attnT[:, 0:2, :].rearrange("p s t -> p (s t)")
        cb_raw = attnT[:, 2:4, :].rearrange("p s t -> p (s t)")[:, 0:C_BF]
        x_norm = probs[:, 0:2, :].rearrange("p a (t d) -> p (a t) d", d=HID)
        x2T = raw[:, 0:2, :]
        gz = sb("gz", [128, 2, 4, NE])
        gex = sb("gex", [128, 2, 4, NE])
        gcmp, geq = (recip[:, n * 256:n * 256 + 256].rearrange("p (t e j) -> p t e j", e=NE, j=NE) for n in range(2))
        grank = sb("grank", [128, 4, NE])
        gsum = sb("gsum", [128, 4])
        gpart = psums[:, 0, 0, :].bitcast(BF16).rearrange("p (c t k) -> p c t k", c=2, t=4)
        combT = attnT[:, 7, 0:HALF].bitcast(BF16).rearrange("p (c t) -> p c t", c=2)

        score = [bank(f"score{i}") for i in range(E_RING)]
        block_max = [bank(f"block_max{i}") for i in range(M_RING)]
        o_bank = [bank(f"o_bank{i}") for i in range(2)]
        m_bank = bank("m_bank")
        gate_bank = [score[2], m_bank]

        cb_ready = sem("cb_ready")
        consts_in, w_in, ffn_w_in, x_loaded, out_stored = map(sem, ("consts_in", "w_in", "ffn_w_in", "x_loaded", "out_stored"))
        w_high, w_split, zeroed = map(sem, ("w_high", "w_split", "zeroed"))
        slab_a_in, slab_b_in, k_copied = map(sem, ("slab_a_in", "slab_b_in", "k_copied"))
        v_in = [sem(f"v_in{p}") for p in range(2)]
        var_ready, dev_ready = sem("var_ready"), sem("dev_ready")
        ln_step, ln_done, x_turned, x_high, x_split, v_proj, v_kept = map(sem, (
            "ln_step", "ln_done", "x_turned", "x_high", "x_split", "v_proj", "v_kept"))
        score_full, score_read = sem("score_full"), sem("score_read")
        max_full, max_read = sem("max_full"), sem("max_read")
        max_step, max_ready, max_row, max_kept = map(sem, ("max_step", "max_ready", "max_row", "max_kept"))
        pv_done, p_added, sum_done, recip_done, o_kept = map(sem, ("pv_done", "p_added", "sum_done", "recip_done", "o_kept"))
        swapped, sin_done, rope_sum, rope_high, rope_low = map(sem, (
            "swapped", "sin_done", "rope_sum", "rope_high", "rope_low"))
        wo_done, mid_step, mid_done, x2_turned, x2_kept = map(sem, ("wo_done", "mid_step", "mid_done", "x2_turned", "x2_kept"))
        lin0_done, h_kept, swi1_done, a_kept, h1_kept = map(sem, ("lin0_done", "h_kept", "swi1_done", "a_kept", "h1_kept"))
        gate_done, gate_z, gate_exp, gate_step, gate_parts, gate_turned, comb_kept = map(sem, (
            "gate_done", "gate_z", "gate_exp", "gate_step", "gate_parts", "gate_turned", "comb_kept"))
        ex_full, ex_g, ex_gu, ex_guc, ex_y, y_kept = map(sem, ("ex_full", "ex_g", "ex_gu", "ex_guc", "ex_y", "y_kept"))
        lin1_done, h3_kept, swi2_done, a2_kept, hf_kept, hf_turned, out_step, out_ready = map(sem, (
            "lin1_done", "h3_kept", "swi2_done", "a2_kept", "hf_kept", "hf_turned", "out_step", "out_ready"))

        def groups(eng, body):
            with eng.Fori(0, HKV - 1) as g:
                body(g, False)
            body(HKV - 1, True)

        items = [(k, c) for k in [8, 9] + list(range(NE)) for c in range(2)]
        CB_FIRST = 4
        NI = len(items)

        block = ctx.enter_context(nc.Block())

        @block.sync
        def _(sp):
            x_v = io["x"].rearrange("b (n p) d -> b p n d", p=128)
            sp.sem_inc(out_stored, 16)
            sp.sem_inc(k_copied, 48)
            out_v = out.rearrange("b (n p) d -> b p n d", p=128)
            sp.dma_start(x_in[:], x_v[0]).then_inc(x_loaded, 16)
            sp.dma_start(cf[:], io["cf"]).then_inc(consts_in, 16)
            sp.dma_start(cb_raw, io["cb"]).then_inc(consts_in, 16)
            wr = w_raw[:, 0:HKV * 384].rearrange("p (g n) -> p g n", g=HKV)
            wk = io["wk"].rearrange("p (g d) -> p g d", g=HKV)
            sp.dma_start(wr[:, :, 0:64], wk).then_inc(w_in, 16)
            sp.dma_start(wr[:, :, 64:128], wk).then_inc(w_in, 16)
            sp.dma_start(wr[:, :, 128:384], io["wq"].rearrange("p (g n) -> p g n", g=HKV)).then_inc(w_in, 16)
            sp.dma_start(w_raw[:, HKV * 384:HKV * 384 + 256], io["wv"]).then_inc(w_in, 16)
            loads = [(w_o[:], io["wo"].rearrange("(s p) n -> p s n", p=128)), (w_lin0[:], io["lin0_w"]),
                     (w_lin1[:], io["lin1_w"]), (gate_wT[:], io["gate_wT"])]
            loads += [(w_swi[:, n, :], io[name]) for n, name in enumerate(("swi1_w1", "swi1_w2", "swi2_w1", "swi2_w2"))]
            loads += [(w_exp[:, n, 0:NE, :], io[name].rearrange("e d h -> d e h"))
                      for n, name in enumerate(("exp_w1", "exp_w3", "exp_w2"))]
            loads += [(w_exp[:, n, NE:, :], io[name].rearrange("d (a h) -> d a h", a=2))
                      for n, name in enumerate(("sh_w1", "sh_w3"))]
            loads += [(w_exp[:, 2, NE:, :], io["sh_w2"].rearrange("(a h) d -> h a d", a=2))]
            loads += [(biases[:, n:n + 1], io[name].rearrange("(d a) -> d a", a=1)) for n, name in enumerate(
                ("lin0_b", "swi1_b1", "swi1_b2", "lin1_b", "swi2_b1", "swi2_b2"))]
            assert len(loads) == FFN_LOADS
            for dst, src in loads:
                sp.dma_start(dst, src).then_inc(ffn_w_in, 16)
            sp.wait_ge(w_split, 1)

            def move(dst, src):
                return sp.dma_start(dst.bitcast(F32), src.bitcast(F32))

            def copy_keys(b, g):
                sp.wait_ge(rope_low, rope_index(b, g, 2) + 2)
                for dst, src in ((kk[1], kk[0]), (kl[1][0], kl[0][0]), (kl[1][1], kl[0][1])):
                    move(dst[:], src[:]).then_inc(k_copied, 16)

            def batch(b, last):
                sp.wait_ge(score_read, b * SCORES_B + E_RING)
                move(slab_a[:], w_qk[:, :, 0, 0:256]).then_inc(slab_a_in, 16)
                move(slab_b[:], w_qk[:, :, 0, 256:384]).then_inc(slab_b_in, 16)
                sp.wait_ge(v_kept, 4 * b + 4)
                for p in range(2):
                    sp.dma_start(v_g[p][:], v_all[:, :, 0:D]).then_inc(v_in[p], 16)
                copy_keys(b, 0)
                with sp.Fori(0, HKV - 1) as g:
                    nx = g + 1
                    sp.wait_ge(score_full, project_index(b, g, ROPES_G - 1) + 1)
                    for slab, n0, n1, there in ((slab_a, 0, 256, slab_a_in), (slab_b, 256, 384, slab_b_in)):
                        move(slab[:], w_qk[:, :, bass.ds(nx, 1), n0:n1].rearrange("p a o n -> p a (o n)")
                                     ).then_inc(there, 16)
                    for p in range(2):
                        sp.wait_ge(pv_done, prob_index(b, g, p, 0, PROBS_P) + P_RING)
                        sp.dma_start(v_g[p][:], v_all[:, :, bass.ds(nx * D, D)]).then_inc(v_in[p], 16)
                    copy_keys(b, nx)
                sp.wait_ge(mid_done, 2 * b + 2)
                if not last:
                    sp.dma_start(x_in[:], one(x_v, b + 1)).then_inc(x_loaded, 16)
                sp.wait_ge(out_ready, 2 * b + 2)
                sp.dma_start(one(out_v, b), x_mid[:]).then_inc(out_stored, 16)

            def one(v, b):
                return v[bass.ds(b, 1), :, :, :].rearrange("o p n d -> (o p) n d")

            with sp.Fori(0, B - 1) as b:
                batch(b, False)
            batch(B - 1, True)
            sp.wait_ge(out_stored, 16 * B + 16)

        @block.tensor
        def _(pe):
            mm = nc.tensor.matmul
            pe.sem_inc(pv_done, P_RING)
            pe.sem_inc(sum_done, 2)

            def split_product(dst, w, x, done=None):
                mm(dst, w[0], x[0], start=True, stop=False)
                mm(dst, w[1], x[0], start=False, stop=False)
                ins = mm(dst, w[0], x[1], start=False, stop=True)
                if done is not None:
                    ins.then_inc(done, 1)

            def project(b, g, k):
                n, c = k // 2, k % 2
                i = project_index(b, g, k)
                if k in (0, PROJ_A):
                    pe.wait_ge(slab_a_in if k == 0 else slab_b_in, 16 * (b * HKV + g + 1))
                pe.wait_ge(score_read, i + 1)
                w = [slab_a[:, a, n * 128:n * 128 + 128] if k < PROJ_A else slab_b[:, a, :] for a in range(2)]
                x = [xT[:, a, c * HALF:c * HALF + HALF] for a in range(2)]
                split_product(score[k % E_RING][:, :], w, x, score_full)

            def block_scores(b, g, p, c, n):
                h, i, kh, width = pieces(c)[n]
                q = prob_index(b, g, p, c, n)
                if c == 0 and n == 0:
                    pe.wait_ge(rope_low, rope_index(b, g, PROJ_A if p == 0 else ROPES_G) + 2)
                    if p == 1:
                        pe.wait_ge(k_copied, 48 * (b * HKV + g + 2))
                pe.wait_ge(max_read, q + 1)
                dst, whole = block_max[n % M_RING], 256 if width <= 256 else HALF
                diagonal = kh == c
                ins = mm(dst[:, 0:whole], qa[p][h][:, i * 128:i * 128 + 128], kk[p][:, kh * HALF:kh * HALF + whole],
                         start=True, stop=not diagonal)
                if diagonal:
                    ins = mm(dst[:, width - 128:width], identb, tri_q, start=False, stop=True)
                ins.then_inc(max_full, 1)

            def max_rows(b, g, p, c):
                v = unit_index(b, g, p, c)
                pe.wait_ge(max_ready, v + 1)
                pe.wait_ge(recip_done, v + 1)
                for h in range(2):
                    r = 64 * (1 - h)
                    for i in range(4):
                        ins = mm(m_bank[r:r + 2, i * 128:i * 128 + 128], neg_max[:, c, h, i, :], identb,
                                 start=True, stop=True)
                ins.then_inc(max_row, 1)

            def sums(b, g, p, c, last):
                v = unit_index(b, g, p, c)
                pe.wait_ge(p_added, prob_index(b, g, p, c, PROBS_U[c]) + P_RING)
                if not (last and p and c):
                    pe.wait_ge(max_kept, v + 2)
                pe.wait_ge(recip_done, v + 2)
                for h in range(2):
                    ins = mm(m_bank[64 * h:64 * h + 64, :], ones, psums[:, c, h, :], start=True, stop=True)
                ins.then_inc(sum_done, 1)

            def unit(b, g, p, c, last, first_item):
                steps = 4 * (c + 1)
                plan = piece_plan(c)
                v = unit_index(b, g, p, c)
                for j in range(steps + LAG):
                    if j < steps:
                        off = max(0, j - 4 * c) * 128
                        even = off // 256 * 256
                        for h in range(2):
                            k = c * PROBS_U[0] + 2 * j + h
                            if j == 0 and h == 0:
                                pe.wait_ge(max_kept, v + 1)
                            pe.wait_ge(score_read, score_index(b, g, p, k, last) + 1)
                            dst = score[(first_item + k) % E_RING]
                            cols = slice(c * HALF + even, c * HALF + HALF)
                            mm(dst[:, even:], kk[p][:, j * 128:j * 128 + 128], qa[p][h][:, cols], start=True, stop=False)
                            ins = mm(dst[:, even:], kl[p][h][:, j * 128:j * 128 + 128], qb[p][h][:, cols],
                                     start=False, stop=j < 4 * c)
                            if j >= 4 * c:
                                ins = mm(dst[:, off:off + 128], identb, tri_k, start=False, stop=True)
                            ins.then_inc(score_full, 1)
                        for ahead, cc, n in plan[j]:
                            if not ahead:
                                block_scores(b, g, p, cc, n)
                            elif p == 0:
                                block_scores(b, g, 1, cc, n)
                            elif not last:
                                block_scores(b, g + 1, 0, cc, n)
                    if j == 2 and (p, c) != (0, 0):
                        sums(b, g, *((p, 0) if c else (0, 1)), last)
                    if j == steps - 1:
                        if c == 0:
                            max_rows(b, g, p, 1)
                        elif p == 0:
                            max_rows(b, g, 1, 0)
                        elif not last:
                            max_rows(b, g + 1, 0, 0)
                    if j >= LAG:
                        t = j - LAG
                        off = max(0, t - 4 * c) * 128
                        if t == 0:
                            pe.wait_ge(o_kept, v + 1)
                            if c == 0:
                                pe.wait_ge(v_in[p], 16 * (b * HKV + g + 1))
                        for h in range(2):
                            k = c * PROBS_U[0] + 2 * t + h
                            pe.wait_ge(score_read, score_index(b, g, p, k, last) + 1 + E_RING)
                            mm(o_bank[c][64 * h:64 * h + 64, off:], v_g[p][:, t, :], probs[:, k % P_RING, off:],
                               start=(t == 0), stop=(t == steps - 1)).then_inc(pv_done, 1)

            def group(b, g, last):
                for p in range(2):
                    first_item = ROPES_G + p * (PROBS_P + (0 if last else PROJ_A))
                    for c in range(2):
                        unit(b, g, p, c, last, first_item)
                    if not last:
                        for k in (range(PROJ_A) if p == 0 else range(PROJ_A, ROPES_G)):
                            project(b, g + 1, k)
                sums(b, g, 1, 1, last)

            pe.wait_ge(consts_in, 32)
            pe.wait_ge(cb_ready, 1)
            pe.wait_ge(zeroed, 2)
            with pe.Fori(0, B) as b:
                for t in range(TILES):
                    pe.wait_ge(ln_done, TILES * b + t + 1)
                    ins = nc.tensor.transpose(block_max[t // 4][:, t % 4 * 128:t % 4 * 128 + 128], x_norm[:, t, :], ident)
                    if t % 4 == 3:
                        ins.then_inc(x_turned, 1)
                pe.wait_ge(x_split, 2 * b + 2)
                for k in range(ROPES_G):
                    project(b, 0, k)
                for t in range(TILES):
                    u = t // 2
                    if t % 2 == 0 and u >= 2:
                        pe.wait_ge(v_kept, 4 * b + u - 1)
                    split_product(o_bank[u % 2][:, t % 2 * 256:t % 2 * 256 + 256],
                                  [xT[:, a, t * 128:t * 128 + 128] for a in range(2)], [w_v[:, a, :] for a in range(2)],
                                  v_proj if t % 2 else None)
                pe.wait_ge(v_kept, 4 * b + 4)
                for n in range(PROBS_U[0]):
                    block_scores(b, 0, 0, 0, n)
                for n in range(EARLY):
                    block_scores(b, 0, 0, 1, n)
                max_rows(b, 0, 0, 0)
                groups(pe, lambda g, last: group(b, g, last))

                pe.wait_ge(ffn_w_in, 16 * FFN_LOADS)
                pe.wait_ge(o_kept, UNITS * b + UNITS + 2)
                for t in range(TILES):
                    for s in range(NP):
                        ins = mm(o_bank[t // 4][:, t % 4 * 128:t % 4 * 128 + 128], attnT[:, s, t * 128:t * 128 + 128],
                                 w_o[:, s, :], start=(s == 0), stop=(s == NP - 1))
                    if t % 4 == 3:
                        ins.then_inc(wo_done, 1)
                for t in range(TILES):
                    if t == 0:
                        pe.wait_ge(mid_done, 2 * b + 2)
                    ins = nc.tensor.transpose(block_max[t // 4][:, t % 4 * 128:t % 4 * 128 + 128], x_norm[:, t, :], ident)
                    if t % 4 == 3:
                        ins.then_inc(x2_turned, 1)

                for c in range(2):
                    pe.wait_ge(x2_kept, 2 * b + c + 1)
                    mm(score[c][:, :], w_lin0[:], x2T[:, c, :], start=True, stop=True).then_inc(lin0_done, 1)
                for c in range(2):
                    pe.wait_ge(h_kept, 2 * b + c + 1)
                    if c == 0:
                        pe.wait_ge(x2_kept, 2 * b + 2)
                    mm(score[c][:, :], w_swi[:, 0, :], hT[:, c, :], start=True, stop=True)
                    mm(block_max[c][:, :], w_swi[:, 1, :], hT[:, c, :], start=True, stop=True).then_inc(swi1_done, 1)
                for c in range(2):
                    pe.wait_ge(h1_kept, 2 * b + c + 1)
                    for t in range(4):
                        ins = mm(gate_bank[c][:, t * NE:t * NE + NE], h1T[:, c, t * 128:t * 128 + 128], gate_wT[:],
                                 start=True, stop=True)
                    ins.then_inc(gate_done, 1)
                for i in range(NI + 2):
                    if i == CB_FIRST - 1:
                        for c in range(2):
                            pe.wait_ge(gate_parts, 2 * b + c + 1)
                            for t in range(4):
                                ins = nc.tensor.transpose(gate_bank[c][:, :].bitcast(BF16)[:, t * 128:t * 128 + 128],
                                                          gpart[:, c, t, :], identb)
                            ins.then_inc(gate_turned, 1)
                    if i < NI:
                        k, c = items[i]
                        if i >= 2:
                            pe.wait_ge(ex_g, NI * b + i - 1)
                            pe.wait_ge(ex_gu, NI * b + i - 1)
                        mm(score[c][:, :], w_exp[:, 0, k, :], h1T[:, c, :], start=True, stop=True)
                        ins = mm(block_max[c][:, :], w_exp[:, 1, k, :], h1T[:, c, :], start=True, stop=True)
                        if k < NE:
                            r = i - CB_FIRST
                            pe.wait_ge(comb_kept, 2 * b + c + 1)
                            if r >= 2:
                                pe.wait_ge(ex_guc, (NI - CB_FIRST) * b + r - 1)
                            ins = mm(gate_bank[c][:, :], cb[:, C_SEL + k * 128:C_SEL + k * 128 + 128], combT[:, c, :],
                                     start=True, stop=True)
                        ins.then_inc(ex_full, 1)
                    if i >= 2:
                        k, c = items[i - 2]
                        if k < NE:
                            pe.wait_ge(ex_guc, (NI - CB_FIRST) * b + i - 2 - CB_FIRST + 1)
                        else:
                            pe.wait_ge(ex_gu, NI * b + i - 1)
                        mm(o_bank[c][:, :], w_exp[:, 2, k, :], (gucT if k < NE else guT)[:, c, :],
                           start=(i - 2 < 2), stop=(i - 2 >= NI - 2)).then_inc(ex_y, 1)
                for c in range(2):
                    pe.wait_ge(y_kept, 2 * b + c + 1)
                    mm(score[c][:, :], w_lin1[:], yT[:, c, :], start=True, stop=True).then_inc(lin1_done, 1)
                for c in range(2):
                    pe.wait_ge(h3_kept, 2 * b + c + 1)
                    mm(score[c][:, :], w_swi[:, 2, :], hT[:, c, :], start=True, stop=True)
                    mm(block_max[c][:, :], w_swi[:, 3, :], hT[:, c, :], start=True, stop=True).then_inc(swi2_done, 1)
                for c in range(2):
                    pe.wait_ge(hf_kept, 2 * b + c + 1)
                    for t in range(4):
                        ins = nc.tensor.transpose(gate_bank[c][:, t * 128:t * 128 + 128],
                                                  h1T[:, c, t * 128:t * 128 + 128], ident)
                    ins.then_inc(hf_turned, 1)

        @block.scalar
        def _(act):
            A = nc.scalar.activation
            act.sem_inc(score_read, E_RING)

            def keep_raw(b, g, k):
                i, r = project_index(b, g, k), rope_index(b, g, k)
                before = 2 if k < 2 else 6 if k < PROJ_A else 4
                act.wait_ge(score_full, i + 1)
                act.wait_ge(swapped, r - before + 1 + ROPES_G)
                A(raw[:, k % 4, :], score[k % E_RING][:, :], ACT.Copy).then_inc(score_read, 1)

            def keep_high(b, g, k):
                r, c = rope_index(b, g, k), k % 2
                cols = slice(c * HALF, c * HALF + HALF)
                act.wait_ge(rope_sum, r + 1)
                if k < 2:
                    act.wait_ge(k_copied, 48 * (b * HKV + g + 1))
                    A(kk[0][:, cols], roped[:, c, :], ACT.Copy).then_inc(rope_high, 1)
                    return
                p = 0 if k < PROJ_A else 1
                for dst in (qa, qb):
                    for h in range(2):
                        ins = A(dst[p][h][64 * h:64 * h + 64, cols], roped[64 * h:64 * h + 64, c, :], ACT.Copy)
                ins.then_inc(rope_high, 1)

            def keep_max(b, g, p, c):
                v = unit_index(b, g, p, c)
                cols = slice(c * HALF, c * HALF + HALF)
                act.wait_ge(max_row, v + 1)
                A(qb[p][0][64:66, cols], m_bank[64:66, :], ACT.Copy)
                A(qb[p][1][0:2, cols], m_bank[0:2, :], ACT.Copy).then_inc(max_kept, 1)

            def deviations(b, n, first, count):
                act.wait_ge(var_ready, NORMS * b + n + 1)
                A(dev[:, first:first + count], mean_var[:, first:first + count, 1], ACT.Sqrt,
                  bias=cf[:, C_EPS:C_EPS + 1]).then_inc(dev_ready, 1)

            def unit(b, g, p, c, last, first_item):
                steps = 4 * (c + 1)
                for j in range(steps):
                    for stage, k in ROPE_PLAN.get((p, c, j), []):
                        if stage == "low" and not (p == 1 and last):
                            keep_high(b, g + p, k)
                    off = max(0, j - 4 * c) * 128
                    for h in range(2):
                        k = c * PROBS_U[0] + 2 * j + h
                        m = prob_index(b, g, p, 0, k)
                        act.wait_ge(score_full, score_index(b, g, p, k, last) + 1)
                        act.wait_ge(pv_done, m + 1)
                        act.wait_ge(p_added, m + 1)
                        A(probs[:, k % P_RING, off:], score[(first_item + k) % E_RING][:, off:], ACT.Exp,
                          scale=float(D) ** -0.5).then_inc(score_read, 1)
                if c == 0:
                    keep_max(b, g, p, 1)
                elif p == 0:
                    keep_max(b, g, 1, 0)
                elif not last:
                    keep_max(b, g + 1, 0, 0)

            def group(b, g, last):
                for p in range(2):
                    first_item = ROPES_G + p * (PROBS_P + (0 if last else PROJ_A))
                    for c in range(2):
                        unit(b, g, p, c, last, first_item)
                    if not last:
                        for k in (range(PROJ_A) if p == 0 else range(PROJ_A, ROPES_G)):
                            keep_raw(b, g + 1, k)

            act.wait_ge(consts_in, 32)
            A(cb[:], cb_raw, ACT.Copy).then_inc(cb_ready, 1)
            act.wait_ge(w_in, 64)
            wr = w_raw[:, 0:HKV * 384].rearrange("p (g n) -> p g n", g=HKV)
            A(w_qk[:, 0, :, :], wr, ACT.Copy)
            A(w_v[:, 0, :], w_raw[:, HKV * 384:HKV * 384 + 256], ACT.Copy).then_inc(w_high, 1)

            act.wait_ge(consts_in, 32)
            with act.Fori(0, B) as b:
                deviations(b, 0, 0, TILES)
                for a in range(2):
                    act.wait_ge(x_turned, 2 * b + a + 1)
                    A(xT[:, 0, a * HALF:a * HALF + HALF], block_max[a][:, :], ACT.Copy).then_inc(x_high, 1)
                for k in range(ROPES_G):
                    if k == PROJ_A:
                        for kh in range(2):
                            keep_high(b, 0, kh)
                    keep_raw(b, 0, k)
                for u in range(4):
                    act.wait_ge(v_proj, 4 * b + u + 1)
                    A(v_all[:, 2 * u:2 * u + 2, :], o_bank[u % 2][:, :].rearrange("p (t n) -> p t n", t=2),
                      ACT.Copy).then_inc(v_kept, 1)
                for k in range(2, PROJ_A):
                    keep_high(b, 0, k)
                keep_max(b, 0, 0, 0)
                groups(act, lambda g, last: group(b, g, last))

                act.wait_ge(ffn_w_in, 16 * FFN_LOADS)
                for a in range(2):
                    deviations(b, 1 + a, 4 * a, 4)
                deviations(b, 3, 0, TILES)
                for c in range(2):
                    act.wait_ge(x2_turned, 2 * b + c + 1)
                    A(x2T[:, c, :], block_max[c][:, :], ACT.Copy).then_inc(x2_kept, 1)
                for c in range(2):
                    act.wait_ge(lin0_done, 2 * b + c + 1)
                    A(hT[:, c, :], score[c][:, :], ACT.Identity, bias=biases[:, 0:1]).then_inc(h_kept, 1)
                for c in range(2):
                    act.wait_ge(swi1_done, 2 * b + c + 1)
                    A(aT[:, c, :], score[c][:, :], ACT.Silu, bias=biases[:, 1:2]).then_inc(a_kept, 1)
                for c in range(2):
                    act.wait_ge(gate_z, 2 * b + c + 1)
                    A(gex[:, c, :, :], gz[:, c, :, :], ACT.Exp).then_inc(gate_exp, 1)
                for i in range(NI):
                    c = items[i][1]
                    if i == CB_FIRST:
                        for cc in range(2):
                            act.wait_ge(gate_turned, 2 * b + cc + 1)
                            A(combT[:, cc, :], gate_bank[cc][:, :].bitcast(BF16)[:, 0:HALF], ACT.Copy).then_inc(comb_kept, 1)
                    act.wait_ge(ex_full, NI * b + i + 1)
                    if i >= 2:
                        act.wait_ge(ex_gu, NI * b + i - 1)
                    A(gT[:, c, :], score[c][:, :], ACT.Silu).then_inc(ex_g, 1)
                for c in range(2):
                    act.wait_ge(ex_y, NI * b + NI - 1 + c)
                    A(yT[:, c, :], o_bank[c][:, :], ACT.Copy).then_inc(y_kept, 1)
                for c in range(2):
                    act.wait_ge(lin1_done, 2 * b + c + 1)
                    A(hT[:, c, :], score[c][:, :], ACT.Identity, bias=biases[:, 3:4]).then_inc(h3_kept, 1)
                for c in range(2):
                    act.wait_ge(swi2_done, 2 * b + c + 1)
                    A(aT[:, c, :], score[c][:, :], ACT.Silu, bias=biases[:, 4:5]).then_inc(a2_kept, 1)
                for c in range(2):
                    deviations(b, 4 + c, 4 * c, 4)

        @block.gpsimd
        def _(pool):
            pool.sem_inc(p_added, P_RING)
            for p in range(2):
                for h in range(2):
                    r = 64 * (1 - h)
                    pool.memset(kl[p][h][:].bitcast(F32), 0.0)
                    ins = pool.memset(qb[p][h][:].bitcast(F32), 0.0)
            ins.then_inc(zeroed, 1)
            pool.wait_ge(zeroed, 1)
            for p in range(2):
                for h in range(2):
                    r = 64 * (1 - h)
                    ins = pool.memset(kl[p][h][r:r + 2, :].bitcast(F32), 1.0)
            ins.then_inc(zeroed, 1)
            pool.wait_ge(consts_in, 32)

            def turn(b, g, k):
                r, c = rope_index(b, g, k), k % 2
                pool.wait_ge(swapped, r + 1 + ROPES_G)
                pool.tensor_tensor(turned[:, c, :], turned[:, c, :], cf[:, C_SIN + c * HALF:C_SIN + c * HALF + HALF],
                                   ALU.mult).then_inc(sin_done, 1)

            def unit(b, g, p, c, last):
                for j in range(4 * (c + 1)):
                    for stage, k in ROPE_PLAN.get((p, c, j), []):
                        if stage == "turn" and not (p == 1 and last):
                            turn(b, g + p, k)
                    if j == 0:
                        continue
                    off = max(0, j - 4 * c) * 128
                    for h in range(2):
                        k = c * PROBS_U[0] + 2 * j + h
                        m = prob_index(b, g, p, 0, k)
                        dst = psums[:, c, h, off:]
                        pool.wait_ge(score_read, score_index(b, g, p, k, last) + 1 + E_RING)
                        if j == 1:
                            if h == 0:
                                pool.wait_ge(sum_done, unit_index(b, g, p, c) + 1)
                            ins = pool.tensor_tensor(dst, probs[:, (k - 2) % P_RING, off:], probs[:, k % P_RING, off:],
                                                     ALU.add)
                            if off:
                                ins = pool.tensor_copy(psums[:, c, h, 0:off], probs[:, (k - 2) % P_RING, 0:off])
                            ins.then_inc(p_added, 3 if h else 1)
                        else:
                            pool.wait_ge(p_added, m - 1 + P_RING)
                            pool.tensor_tensor(dst, dst, probs[:, k % P_RING, off:], ALU.add).then_inc(p_added, 1)

            def group(b, g, last):
                for p in range(2):
                    for c in range(2):
                        unit(b, g, p, c, last)

            with pool.Fori(0, B) as b:
                for k in range(PROJ_A):
                    turn(b, 0, k)
                groups(pool, lambda g, last: group(b, g, last))

        @block.vector
        def _(dve):
            V = nc.vector
            dve.sem_inc(max_read, M_RING)
            dve.sem_inc(recip_done, 2)
            dve.sem_inc(o_kept, 2)
            dve.sem_inc(swapped, ROPES_G)
            dve.sem_inc(rope_low, 2)

            class Steps:
                def __init__(self, b):
                    self.b, self.base, self.n, self.deviations = b, b * STEPS_B, 0, 0

                def __call__(self, ins):
                    self.n += 1
                    ins.then_inc(ln_step, 1)
                    dve.wait_ge(ln_step, self.base + self.n)

            def statistics(step, src, tiles):
                n = len(tiles)
                for t in tiles:
                    ins = V.bn_stats(stats[:, t, :], src(t))
                step(ins)
                V.memset(unused[:], 0.0)
                for t in tiles:
                    ins = V.bn_aggr(mean_var[:, t, :], stats[:, t, :])
                step.deviations += 1
                ins.then_inc(var_ready, 1)
                dve.wait_ge(dev_ready, NORMS * step.b + step.deviations)
                step(V.reciprocal(rstd[:, tiles[0]:tiles[0] + n], dev[:, tiles[0]:tiles[0] + n]))

            def normalise(dst, src, t):
                return V.tensor_scalar(dst, src, mean_var[:, t, 0:1], rstd[:, t:t + 1], ALU.subtract, ALU.mult)

            def rope_work(b, g, stage, k):
                r, c = rope_index(b, g, k), k % 2
                cols = slice(c * HALF, c * HALF + HALF)
                if stage == "turn":
                    dve.wait_ge(rope_low, r + 1)
                    dve.wait_ge(score_read, project_index(b, g, k) + 1 + E_RING)
                    V.tensor_tensor(roped[:, c, :], raw[:, k % 4, :], cf[:, C_COS + c * HALF:C_COS + c * HALF + HALF],
                                    ALU.mult)
                    V.stream_shuffle(turned[:, c, :], raw[:, k % 4, :], SWAP).then_inc(swapped, 1)
                elif stage == "sum":
                    dve.wait_ge(sin_done, r + 1)
                    dve.wait_ge(swapped, r + 1 + ROPES_G)
                    V.tensor_tensor(roped[:, c, :], roped[:, c, :], turned[:, c, :], ALU.add).then_inc(rope_sum, 1)
                else:
                    dve.wait_ge(rope_high, r + 1)
                    for h in range(2):
                        half = slice(64 * h, 64 * h + 64)
                        if k < 2:
                            ins = V.tensor_tensor(kl[0][h][half, cols], roped[half, c, :], kk[0][half, cols], ALU.subtract)
                        else:
                            p = 0 if k < PROJ_A else 1
                            ins = V.tensor_tensor(qa[p][h][64 * (1 - h):64 * (1 - h) + 64, cols], roped[half, c, :],
                                                  qb[p][h][half, cols], ALU.subtract)
                    ins.then_inc(rope_low, 1)

            def block_maximum(b, g, p, c, n):
                h, i, kh, width = pieces(c)[n]
                q = prob_index(b, g, p, c, n)
                dve.wait_ge(max_full, q + 1)
                V.reduce_max(maxes[:, c, h, kh, i % 4:i % 4 + 1], block_max[n % M_RING][:, 0:width], AX_X
                             ).then_inc(max_read, 1)
                if n == PROBS_U[c] - 1:
                    negate(b, g, p, c)

            def negate(b, g, p, c):
                v = unit_index(b, g, p, c)
                m0 = (b * NP + g * 2 + p) * 3 + c
                dve.wait_ge(max_read, prob_index(b, g, p, c, PROBS_U[c]) + M_RING)
                top_v = maxes[:, 0, :, 0, :]
                if c:
                    V.tensor_tensor(top[:], maxes[:, 1, :, 0, :], maxes[:, 1, :, 1, :], ALU.max).then_inc(max_step, 1)
                    dve.wait_ge(max_step, m0 + 1)
                    top_v, m0 = top[:], m0 + 1
                V.tensor_scalar(neg_max[:, c, :, :, 0], top_v, -1.0, None, ALU.mult).then_inc(max_step, 1)
                dve.wait_ge(max_step, m0 + 1)
                V.scalar_tensor_tensor(out=neg_max[:, c, :, :, 1], in0=top_v, scalar=-1.0, in1=neg_max[:, c, :, :, 0],
                                       op0=ALU.mult, op1=ALU.subtract).then_inc(max_ready, 1)

            def divide(b, g, p, c):
                v = unit_index(b, g, p, c)
                dve.wait_ge(o_kept, v + 2)
                dve.wait_ge(sum_done, v + 1 + 2)
                V.reciprocal(recip[:], m_bank[:, :]).then_inc(recip_done, 1)
                dve.wait_ge(recip_done, v + 1 + 2)
                dve.wait_ge(pv_done, prob_index(b, g, p, c, PROBS_U[c]) + P_RING)
                if isinstance(g, int):
                    dst = attnT[:, 2 * g + p, c * HALF:c * HALF + HALF]
                else:
                    dst = attnT[:, bass.ds(2 * g + p, 1), c * HALF:c * HALF + HALF].rearrange("p o t -> p (o t)")
                V.tensor_tensor(dst, o_bank[c][:, :], recip[:], ALU.mult).then_inc(o_kept, 1)

            def unit(b, g, p, c, last):
                plan = piece_plan(c)
                for j in range(4 * (c + 1)):
                    for stage, k in ROPE_PLAN.get((p, c, j), []):
                        if not (p == 1 and last):
                            rope_work(b, g + p, stage, k)
                    for ahead, cc, n in plan[j]:
                        if not ahead:
                            block_maximum(b, g, p, cc, n)
                        elif p == 0:
                            block_maximum(b, g, 1, cc, n)
                        elif not last:
                            block_maximum(b, g + 1, 0, cc, n)
                    if j == 3 and (p, c) != (0, 0):
                        divide(b, g, *((p, 0) if c else (0, 1)))

            def group(b, g, last):
                for p in range(2):
                    for c in range(2):
                        unit(b, g, p, c, last)
                divide(b, g, 1, 1)

            def route(step, b, c):
                ex = gex[:, c, :, :]
                mine = ex.unsqueeze(3).to_broadcast([128, 4, NE, NE])
                other = ex.unsqueeze(2).to_broadcast([128, 4, NE, NE])
                tie = cf[:, C_TIE:C_TIE + 64].rearrange("p (a e j) -> p a e j", a=1, e=NE).to_broadcast([128, 4, NE, NE])
                if c:
                    dve.wait_ge(gate_parts, 2 * b + 1)
                dve.wait_ge(gate_exp, 2 * b + c + 1)
                V.tensor_tensor(gcmp, other, mine, ALU.is_gt)
                step(V.tensor_tensor(geq, other, mine, ALU.is_equal))
                step(V.tensor_tensor(geq, geq, tie, ALU.mult))
                step(V.tensor_tensor(gcmp, gcmp, geq, ALU.add))
                step(V.tensor_reduce(grank[:], gcmp, AX_X, ALU.add))
                step(V.scalar_tensor_tensor(out=grank[:], in0=grank[:], scalar=TOPK - 0.5, in1=ex,
                                            op0=ALU.is_lt, op1=ALU.mult))
                step(V.tensor_reduce(gsum[:], grank[:], AX_X, ALU.add))
                step(V.reciprocal(gsum[:], gsum[:]))
                step(V.tensor_tensor(grank[:], grank[:], gsum[:].unsqueeze(2).to_broadcast([128, 4, NE]), ALU.mult))
                for part in range(3):
                    cols = slice(part * NE, part * NE + NE)
                    ins = V.tensor_copy(gpart[:, c, :, cols], grank[:])
                    if part < 2:
                        step(ins)
                        step(V.tensor_tensor(grank[:], grank[:], gpart[:, c, :, cols], ALU.subtract))
                ins.then_inc(gate_parts, 1)

            dve.wait_ge(w_high, 1)
            wr = w_raw[:, 0:HKV * 384].rearrange("p (g n) -> p g n", g=HKV)
            V.tensor_tensor(w_qk[:, 1, :, :], wr, w_qk[:, 0, :, :], ALU.subtract)
            V.tensor_tensor(w_v[:, 1, :], w_raw[:, HKV * 384:HKV * 384 + 256], w_v[:, 0, :], ALU.subtract).then_inc(w_split, 1)
            dve.wait_ge(zeroed, 2)
            dve.wait_ge(consts_in, 32)

            with dve.Fori(0, B) as b:
                step = Steps(b)
                dve.wait_ge(x_loaded, 16 * (b + 1))
                statistics(step, lambda t: x_in[:, t, :], list(range(TILES)))
                for t in range(TILES):
                    normalise(x_norm[:, t, :], x_in[:, t, :], t).then_inc(ln_done, 1)
                for a in range(2):
                    cols = slice(a * HALF, a * HALF + HALF)
                    dve.wait_ge(x_high, 2 * b + a + 1)
                    V.tensor_tensor(xT[:, 1, cols], block_max[a][:, :], xT[:, 0, cols], ALU.subtract).then_inc(x_split, 1)
                for two in ((0, 1), (2, 3)):
                    for stage in ("turn", "sum", "low"):
                        for k in two:
                            rope_work(b, 0, stage, k)
                for n in range(PROBS_U[0]):
                    block_maximum(b, 0, 0, 0, n)
                for n in range(EARLY):
                    block_maximum(b, 0, 0, 1, n)
                groups(dve, lambda g, last: group(b, g, last))

                dve.wait_ge(out_stored, 16 * b + 16)
                for a in range(2):
                    tiles = list(range(4 * a, 4 * a + 4))
                    dve.wait_ge(wo_done, 2 * b + a + 1)
                    src = lambda t: o_bank[t // 4][:, t % 4 * 128:t % 4 * 128 + 128]
                    statistics(step, src, tiles)
                    for t in tiles:
                        ins = normalise(x_mid[:, t, :], src(t), t)
                    step(ins)
                    V.tensor_tensor(x_mid[:, 4 * a:4 * a + 4, :], x_mid[:, 4 * a:4 * a + 4, :], x_in[:, 4 * a:4 * a + 4, :],
                                    ALU.add).then_inc(mid_step, 1)
                dve.wait_ge(mid_step, 2 * b + 2)
                statistics(step, lambda t: x_mid[:, t, :], list(range(TILES)))
                for t in range(TILES):
                    ins = normalise(x_norm[:, t, :], x_mid[:, t, :], t)
                ins.then_inc(mid_done, 2)

                for c in range(2):
                    dve.wait_ge(a_kept, 2 * b + c + 1)
                    V.scalar_tensor_tensor(out=h1T[:, c, :], in0=block_max[c][:, :], scalar=biases[:, 2:3], in1=aT[:, c, :],
                                           op0=ALU.add, op1=ALU.mult).then_inc(h1_kept, 1)
                for c in range(2):
                    if c:
                        dve.wait_ge(gate_z, 2 * b + 1)
                    dve.wait_ge(gate_done, 2 * b + c + 1)
                    lg = gate_bank[c][:, 0:4 * NE].rearrange("p (t e) -> p t e", e=NE)
                    step(V.tensor_reduce(gsum[:], lg, AX_X, ALU.max))
                    V.tensor_tensor(gz[:, c, :, :], lg, gsum[:].unsqueeze(2).to_broadcast([128, 4, NE]),
                                    ALU.subtract).then_inc(gate_z, 1)
                step(V.memset(psums[:, 0, 0, :], 0.0))
                for i in range(NI):
                    k, c = items[i]
                    if i == 2:
                        route(step, b, 0)
                        route(step, b, 1)
                    dve.wait_ge(ex_g, NI * b + i + 1)
                    if i >= 2:
                        dve.wait_ge(ex_y, NI * b + i - 1)
                    V.tensor_tensor(guT[:, c, :], block_max[c][:, :], gT[:, c, :], ALU.mult).then_inc(ex_gu, 1)
                    if k < NE:
                        dve.wait_ge(ex_gu, NI * b + i + 1)
                        V.tensor_tensor(gucT[:, c, :], gate_bank[c][:, :], guT[:, c, :], ALU.mult).then_inc(ex_guc, 1)
                for c in range(2):
                    dve.wait_ge(a2_kept, 2 * b + c + 1)
                    V.scalar_tensor_tensor(out=h1T[:, c, :], in0=block_max[c][:, :], scalar=biases[:, 5:6], in1=aT[:, c, :],
                                           op0=ALU.add, op1=ALU.mult).then_inc(hf_kept, 1)
                for c in range(2):
                    tiles = list(range(4 * c, 4 * c + 4))
                    dve.wait_ge(hf_turned, 2 * b + c + 1)
                    src = lambda t: gate_bank[t // 4][:, t % 4 * 128:t % 4 * 128 + 128]
                    statistics(step, src, tiles)
                    for t in tiles:
                        ins = normalise(x_norm[:, t, :], src(t), t)
                    step(ins)
                    V.tensor_tensor(x_mid[:, 4 * c:4 * c + 4, :], x_mid[:, 4 * c:4 * c + 4, :],
                                    x_norm[:, 4 * c:4 * c + 4, :], ALU.add).then_inc(out_ready, 1)
                assert step.n == STEPS_B, step.n


def constants():
    cf = np.zeros((128, C_F32), np.float32)
    cf[:, C_ID:C_ID + 128] = np.eye(128)
    cf[:, C_EPS] = EPS
    cf[:, C_ONES:C_ONES + D] = 1.0
    cf[:, C_TIE:C_TIE + 64] = (np.arange(NE)[None, :] < np.arange(NE)[:, None]).reshape(1, 64)
    inv_freq = (np.float32(1.0) / np.float32(ROPE_THETA) ** (np.arange(0, D, 2, dtype=np.float32) / np.float32(D)))
    freqs = np.arange(S, dtype=np.float32)[:, None] * inv_freq.astype(np.float32)[None, :]
    emb = np.concatenate([freqs, freqs], axis=-1)[:, 0::2]
    pair = (np.arange(128) % D) // 2
    sign = np.where(np.arange(128) % 2 == 0, -1.0, 1.0).astype(np.float32)
    cf[:, C_COS:C_COS + S] = np.cos(emb).T[pair]
    cf[:, C_SIN:C_SIN + S] = np.sin(emb).T[pair] * sign[:, None]
    cb = np.zeros((128, C_BF), np.float32)
    cb[:, C_IDB:C_IDB + 128] = np.eye(128)
    at = np.arange(128)
    cb[:, C_TRIQ:C_TRIQ + 128] = np.where(at[None, :] > at[:, None], MASKED, 0.0)
    cb[:, C_TRIK:C_TRIK + 128] = np.where(at[:, None] > at[None, :], MASKED, 0.0)
    for e in range(NE):
        for part in range(3):
            cb[part * NE + e, C_SEL + e * 128:C_SEL + e * 128 + 128] = 1.0
    return cf, cb


_INS = {"x": "L0_attn_hidden_states", "wq": "L0_attn_Wq", "wk": "L0_attn_Wk", "wv": "L0_attn_Wv", "wo": "L0_attn_Wo"}
_INS.update({n: "L0_ffn_" + n for n in (
    "lin0_w", "lin0_b", "swi1_w1", "swi1_b1", "swi1_w2", "swi1_b2", "gate_w", "exp_w1", "exp_w3", "exp_w2",
    "sh_w1", "sh_w3", "sh_w2", "lin1_w", "lin1_b", "swi2_w1", "swi2_b1", "swi2_w2", "swi2_b2")})


def kernel(**inputs):
    import numpy as _np
    import concourse.bacc as _bacc
    from concourse import mybir as _mybir
    from concourse.bass_utils import run_bass_kernel_spmd as _run

    nc = _bacc.Bacc("TRN2", target_bir_lowering=False, num_devices=1)
    arrays = {n: _np.ascontiguousarray(inputs[name]) for n, name in _INS.items()}
    arrays["gate_wT"] = _np.ascontiguousarray(arrays.pop("gate_w").T)
    arrays["cf"], arrays["cb"] = constants()
    io = {n: nc.dram_tensor(f"in_{n}", a.shape, _mybir.dt.from_np(a.dtype), kind="ExternalInput").ap()
          for n, a in arrays.items()}
    out = nc.dram_tensor("out_0", (B, S, HID), F32, kind="ExternalOutput").ap()
    build(nc, io, out)
    r = _run(nc, [{f"in_{n}": a for n, a in arrays.items()}], core_ids=[0])
    return r.results[0]["out_0"]
```

```python
from contextlib import ExitStack

import numpy as np
import concourse.bass as bass
from concourse import mybir

F32 = mybir.dt.float32
F32R = mybir.dt.float32r
BF16 = mybir.dt.bfloat16
ALU = mybir.AluOpType
ACT = mybir.ActivationFunctionType
AX_X = mybir.AxisListType.X

B, S, HID = 4, 1024, 128
HKV, D = 4, 64
PAIRS = 2
NP = HKV * PAIRS
TILES = S // 128
HALF = 512
UNITS = 2 * NP
NE, TOPK = 8, 4
FFN_STEPS = NE + 2
EPS = 1e-5
MASKED = -1e30
ROPE_THETA = 10000.0

E_RING, P_RING, M_RING = 2, 6, 3
LAG = 2

PROJ_A, PROJ_B = 4, 2
ROPES_G = PROJ_A + PROJ_B
ROPES_B = ROPES_G * HKV
PROBS_U = (8, 16)
PROBS_P = sum(PROBS_U)
PROBS_G = PAIRS * PROBS_P
PROBS_B = HKV * PROBS_G
SCORES_G = ROPES_G + PROBS_G + 4
SCORES_B = HKV * SCORES_G
assert SCORES_G % E_RING == 0 and PROBS_P % P_RING == 0 and PROBS_P % M_RING == 0

C_ID, C_ONES, C_TIE, C_COS, C_SIN, C_EPS, C_F32 = 0, 128, 192, 256, 256 + S, 256 + 2 * S, 257 + 2 * S
FFN_LOADS = 20

NORMS = 6
SWAP = [i ^ 1 for i in range(32)]
STEPS_B = 2 + 2 * 3 + 2 + 2 * 1 + 1 + 2 * 12 + 2 * 3
C_IDB, C_TRIQ, C_TRIK, C_SEL, C_BF = 0, 128, 256, 384, 384 + NE * 128


def rope_index(b, g, k):
    return b * ROPES_B + g * ROPES_G + k


def score_item(p, c, k, last=False):
    first = {(0, 0): 0, (0, 1): PROBS_U[0] + 1}
    first[1, 0] = PROBS_P + 2 + (0 if last else PROJ_A)
    first[1, 1] = first[1, 0] + PROBS_U[0] + 1 + (0 if last else PROJ_B)
    return first[p, c] + k


def score_index(b, g, item):
    return b * SCORES_B + ROPES_G + 1 + g * SCORES_G + item


def row_item(p, c, last=False):
    before = {(0, 1): (0, 0), (1, 0): (0, 1), (1, 1): (1, 0), (0, 0): (1, 1)}[p, c]
    return score_item(*before, PROBS_U[before[1]], last and (p, c) != (0, 0))


def row_index(b, g, p, c, last=False):
    return score_index(b, g if (p, c) != (0, 0) else g - 1, row_item(p, c, last))


def project_item(k):
    return PROBS_P + 2 + k if k < PROJ_A else score_item(1, 1, 0) - ROPES_G + k


def project_index(b, g, k):
    if isinstance(g, int) and g == 0:
        return b * SCORES_B + k
    return score_index(b, g - 1, project_item(k))


def bank_of(item):
    return (ROPES_G + 1 + item) % E_RING


def pieces(c):
    out = []
    for h in range(2):
        for i in range(4 * c, 4 * c + 4):
            for kh in range(c + 1):
                out.append((h, i, kh, HALF if kh < c else (i - 4 * c + 1) * 128))
    if c:
        out = [x for h in range(2) for kh in range(2) for x in out if x[0] == h and x[2] == kh]
    return out


EARLY = 3
MAX_PLAN = {
    (0, 0): [(1, 3, 8), (1, 8, 12), (1, 12, 16)],
    (0, 1): [(0, 0, 4), (0, 4, 8), (1, 0, 3), (1, 3, 6), (1, 6, 9), (1, 9, 12), (1, 12, 16)],
    (1, 0): [],
    (1, 1): [(0, 0, 0), (0, 0, 0), (0, 0, 2), (0, 2, 4), (0, 4, 6), (0, 6, 8), (1, 0, 1), (1, 1, 3)],
}


def piece_plan(p, c, j, b, g, last):
    if j >= len(MAX_PLAN[p, c]) or ((p, c) == (1, 1) and last):
        return []
    half, first, end = MAX_PLAN[p, c][j]
    pair = (g, p) if c == 0 else (g, 1) if p == 0 else (g + 1, 0)
    return [(b, *pair, half, n) for n in range(first, end)]


def prob_index(b, g, p, c, n):
    return b * PROBS_B + g * PROBS_G + p * PROBS_P + c * PROBS_U[0] + n


def unit_index(b, g, p, c):
    return b * UNITS + g * 4 + p * 2 + c


ROPE_PLAN = {
    (0, 0, 2): [("low", 4)], (0, 1, 0): [("low", 5)],
    (1, 0, 0): [("turn", 0)], (1, 0, 1): [("turn", 1), ("sum", 0)],
    (1, 0, 2): [("low", 0), ("sum", 1), ("turn", 2)], (1, 0, 3): [("low", 1), ("sum", 2)],
    (1, 1, 0): [("low", 2), ("turn", 3)], (1, 1, 1): [("sum", 3)], (1, 1, 2): [("low", 3)],
    (1, 1, 4): [("turn", 4)], (1, 1, 5): [("sum", 4)], (1, 1, 6): [("turn", 5)], (1, 1, 7): [("sum", 5)],
}


def rope_plan(p, c, j, last):
    if p == 1 and last:
        return []
    return [(stage, p, k) for stage, k in ROPE_PLAN.get((p, c, j), [])]


SUM_STEP = 1
RECIP_STEP = 2
DIVIDE_STEP = (3, 3)


def build(nc, io, out):
    with ExitStack() as ctx:
        def sb(name, shape, dt=F32):
            return ctx.enter_context(nc.sbuf_tensor(name, shape, dt))

        def bank(name):
            return ctx.enter_context(nc.psum_tensor(name, [128, HALF], F32))

        def sem(name):
            return ctx.enter_context(nc.semaphore(name))

        cf = sb("cf", [128, C_F32])
        cb = sb("cb", [128, C_BF], BF16)
        ident, identb = cf[:, C_ID:C_ID + 128], cb[:, C_IDB:C_IDB + 128]
        ones = cf[:, C_ONES:C_ONES + D]
        tri_q, tri_k = cb[:, C_TRIQ:C_TRIQ + 128], cb[:, C_TRIK:C_TRIK + 128]
        biases = sb("biases", [128, 6])
        gate_wT = sb("gate_wT", [128, NE])
        w_lin0, w_lin1 = sb("w_lin0", [128, 128]), sb("w_lin1", [128, 128])
        w_swi = sb("w_swi", [128, 4, 128])
        w_exp = sb("w_exp", [128, 3, FFN_STEPS, 128])
        w_o = sb("w_o", [128, NP, HID])
        w_qk = sb("w_qk", [128, 2, HKV, 384], F32R)
        w_v = sb("w_v", [128, 2, HKV * D], F32R)
        slab_a = sb("slab_a", [128, 2, 256], F32R)
        slab_b = sb("slab_b", [128, 2, 128], F32R)
        x_in = sb("x_in", [128, TILES, HID])
        x_mid = sb("x_mid", [128, TILES, HID])
        stats = sb("stats", [128, TILES, 6])
        mean_var = sb("mean_var", [128, TILES, 2])
        dev = sb("dev", [128, TILES])
        rstd = sb("rstd", [128, TILES])
        unused = sb("unused", [128, 1])
        xT = sb("xT", [128, 2, S], F32R)
        v_all = sb("v_all", [128, TILES, HKV * D])
        v_g = [sb(f"v_g{p}", [128, TILES, D]) for p in range(2)]
        kk = [sb(f"kk{p}", [128, S], F32R) for p in range(2)]
        kl = [[sb(f"kl{p}{h}", [128, S], F32R) for h in range(2)] for p in range(2)]
        qa = [[sb(f"qa{p}{h}", [128, S], F32R) for h in range(2)] for p in range(2)]
        qb = [[sb(f"qb{p}{h}", [128, S], F32R) for h in range(2)] for p in range(2)]
        raw = sb("raw", [128, 4, HALF])
        turned = sb("turned", [128, 2, HALF])
        roped = sb("roped", [128, 2, HALF])
        probs = sb("probs", [128, P_RING, HALF])
        psums = sb("psums", [128, 2, 2, HALF])
        recip = sb("recip", [128, HALF])
        maxes = sb("maxes", [128, 2, 2, 2, 4])
        top = sb("top", [128, 2, 4])
        neg_max = sb("neg_max", [128, 2, 2, 4, 2], BF16)
        attnT = sb("attnT", [128, NP, S])
        def ffn_buf(n):
            return attnT[:, n, :].rearrange("p (c t) -> p c t", c=2)
        hT, aT, h1T, gT, guT, gucT, yT = (ffn_buf(n) for n in range(7))
        w_raw = attnT[:, 0:2, :].rearrange("p s t -> p (s t)")
        cb_raw = attnT[:, 2:4, :].rearrange("p s t -> p (s t)")[:, 0:C_BF]
        x_norm = probs[:, 0:2, :].rearrange("p a (t d) -> p (a t) d", d=HID)
        x2T = raw[:, 0:2, :]
        gz = sb("gz", [128, 2, 4, NE])
        gex = sb("gex", [128, 2, 4, NE])
        gcmp, geq = (recip[:, n * 256:n * 256 + 256].rearrange("p (t e j) -> p t e j", e=NE, j=NE) for n in range(2))
        grank = sb("grank", [128, 4, NE])
        gsum = sb("gsum", [128, 4])
        gpart = psums[:, 0, 0, :].bitcast(BF16).rearrange("p (c t k) -> p c t k", c=2, t=4)
        combT = attnT[:, 7, 0:HALF].bitcast(BF16).rearrange("p (c t) -> p c t", c=2)

        score = [bank(f"score{i}") for i in range(E_RING)]
        block_max = [bank(f"block_max{i}") for i in range(M_RING)]
        o_bank = [bank(f"o_bank{i}") for i in range(2)]
        m_bank = bank("m_bank")
        gate_bank = [block_max[2], m_bank]

        cb_ready = sem("cb_ready")
        consts_in, w_in, ffn_w_in, x_loaded, out_stored = map(sem, ("consts_in", "w_in", "ffn_w_in", "x_loaded", "out_stored"))
        w_high, w_split, zeroed = map(sem, ("w_high", "w_split", "zeroed"))
        slab_a_in, slab_b_in, k_copied, q_copied = map(sem, ("slab_a_in", "slab_b_in", "k_copied", "q_copied"))
        v_in = [sem(f"v_in{p}") for p in range(2)]
        var_ready, dev_ready = sem("var_ready"), sem("dev_ready")
        ln_step, ln_done, x_turned, x_high, x_split, v_proj, v_kept = map(sem, (
            "ln_step", "ln_done", "x_turned", "x_high", "x_split", "v_proj", "v_kept"))
        score_full, score_read = sem("score_full"), sem("score_read")
        max_full, max_read = sem("max_full"), sem("max_read")
        max_step, max_ready = map(sem, ("max_step", "max_ready"))
        pv_done, p_added, sum_done, recip_ready, divide_step, sum_read, o_kept = map(sem, (
            "pv_done", "p_added", "sum_done", "recip_ready", "divide_step", "sum_read", "o_kept"))
        log_done = sem("log_done")
        swapped, sin_done, rope_sum, rope_high, rope_low = map(sem, (
            "swapped", "sin_done", "rope_sum", "rope_high", "rope_low"))
        wo_done, mid_step, mid_done, x2_turned, x2_kept = map(sem, ("wo_done", "mid_step", "mid_done", "x2_turned", "x2_kept"))
        lin0_done, h_kept, swi1_done, a_kept, h1_kept = map(sem, ("lin0_done", "h_kept", "swi1_done", "a_kept", "h1_kept"))
        gate_done, gate_z, gate_exp, gate_step, gate_parts, gate_turned, comb_kept = map(sem, (
            "gate_done", "gate_z", "gate_exp", "gate_step", "gate_parts", "gate_turned", "comb_kept"))
        ex_full, ex_g, ex_gu, ex_guc, ex_y, y_kept = map(sem, ("ex_full", "ex_g", "ex_gu", "ex_guc", "ex_y", "y_kept"))
        lin1_done, h3_kept, swi2_done, a2_kept, hf_kept, hf_turned, out_step, out_ready = map(sem, (
            "lin1_done", "h3_kept", "swi2_done", "a2_kept", "hf_kept", "hf_turned", "out_step", "out_ready"))

        def project_plan(p, c, last):
            return {(0, 1): range(PROJ_A), (1, 0): range(PROJ_A, ROPES_G)}.get((p, c), []) if not last else []

        def i_bank(g, k):
            return k % E_RING if isinstance(g, int) and g == 0 else bank_of(project_item(k))

        def units(eng, unit):
            unit(0, 0, 0, False)
            with eng.Fori(0, HKV - 1) as g:
                for p, c in ((0, 1), (1, 0), (1, 1)):
                    unit(g, p, c, False)
                unit(g + 1, 0, 0, False)
            for p, c in ((0, 1), (1, 0), (1, 1)):
                unit(HKV - 1, p, c, True)

        def before(g, p, c):
            if (p, c) != (0, 0):
                return [(g, *{(0, 1): (0, 0), (1, 0): (0, 1), (1, 1): (1, 0)}[p, c])]
            return [] if isinstance(g, int) and g == 0 else [(g - 1, 1, 1)]

        items = [(k, c) for k in [8, 9] + list(range(NE)) for c in range(2)]
        CB_FIRST = 4
        NI = len(items)

        block = ctx.enter_context(nc.Block())

        @block.sync
        def _(sp):
            x_v = io["x"].rearrange("b (n p) d -> b p n d", p=128)
            sp.sem_inc(out_stored, 16)
            sp.sem_inc(k_copied, 48)
            out_v = out.rearrange("b (n p) d -> b p n d", p=128)
            sp.dma_start(x_in[:], x_v[0]).then_inc(x_loaded, 16)
            sp.dma_start(cf[:], io["cf"]).then_inc(consts_in, 16)
            sp.dma_start(cb_raw, io["cb"]).then_inc(consts_in, 16)
            wr = w_raw[:, 0:HKV * 384].rearrange("p (g n) -> p g n", g=HKV)
            wk = io["wk"].rearrange("p (g d) -> p g d", g=HKV)
            sp.dma_start(wr[:, :, 0:64], wk).then_inc(w_in, 16)
            sp.dma_start(wr[:, :, 64:128], wk).then_inc(w_in, 16)
            sp.dma_start(wr[:, :, 128:384], io["wq"].rearrange("p (g n) -> p g n", g=HKV)).then_inc(w_in, 16)
            sp.dma_start(w_raw[:, HKV * 384:HKV * 384 + 256], io["wv"]).then_inc(w_in, 16)
            loads = [(w_o[:], io["wo"].rearrange("(s p) n -> p s n", p=128)), (w_lin0[:], io["lin0_w"]),
                     (w_lin1[:], io["lin1_w"]), (gate_wT[:], io["gate_wT"])]
            loads += [(w_swi[:, n, :], io[name]) for n, name in enumerate(("swi1_w1", "swi1_w2", "swi2_w1", "swi2_w2"))]
            loads += [(w_exp[:, n, 0:NE, :], io[name].rearrange("e d h -> d e h"))
                      for n, name in enumerate(("exp_w1", "exp_w3", "exp_w2"))]
            loads += [(w_exp[:, n, NE:, :], io[name].rearrange("d (a h) -> d a h", a=2))
                      for n, name in enumerate(("sh_w1", "sh_w3"))]
            loads += [(w_exp[:, 2, NE:, :], io["sh_w2"].rearrange("(a h) d -> h a d", a=2))]
            loads += [(biases[:, n:n + 1], io[name].rearrange("(d a) -> d a", a=1)) for n, name in enumerate(
                ("lin0_b", "swi1_b1", "swi1_b2", "lin1_b", "swi2_b1", "swi2_b2"))]
            assert len(loads) == FFN_LOADS
            for dst, src in loads:
                sp.dma_start(dst, src).then_inc(ffn_w_in, 16)
            sp.wait_ge(w_split, 1)

            def move(dst, src):
                return sp.dma_start(dst.bitcast(F32), src.bitcast(F32))

            def copy_keys():
                move(kk[1][:], kk[0][:]).then_inc(k_copied, 16)
                for dst in (kl[1][0][0:64, :], kl[1][1][64:128, :]):
                    move(dst, kl[0][0][0:64, :]).then_inc(k_copied, 16)

            def copy_queries(b, g, p):
                sp.wait_ge(rope_low, rope_index(b, g, ROPES_G if p else PROJ_A) + 2)
                if p == 0:
                    move(kl[0][1][64:128, :], kl[0][0][0:64, :]).then_inc(q_copied, 16)
                for h in range(2):
                    half = slice(64 * h, 64 * h + 64)
                    move(qb[p][h][half, :], qa[p][h][half, :]).then_inc(q_copied, 16)

            def batch(b, last):
                sp.wait_ge(score_read, b * SCORES_B + E_RING)
                move(slab_a[:], w_qk[:, :, 0, 0:256]).then_inc(slab_a_in, 16)
                move(slab_b[:], w_qk[:, :, 0, 256:384]).then_inc(slab_b_in, 16)
                sp.wait_ge(v_kept, 4 * b + 4)
                for p in range(2):
                    sp.dma_start(v_g[p][:], v_all[:, :, 0:D]).then_inc(v_in[p], 16)
                copy_queries(b, 0, 0)
                copy_keys()
                with sp.Fori(0, HKV - 1) as g:
                    nx = g + 1
                    copy_queries(b, g, 1)
                    for slab, n0, n1, there in ((slab_a, 0, 256, slab_a_in), (slab_b, 256, 384, slab_b_in)):
                        move(slab[:], w_qk[:, :, bass.ds(nx, 1), n0:n1].rearrange("p a o n -> p a (o n)")
                                     ).then_inc(there, 16)
                    for p in range(2):
                        if p:
                            copy_queries(b, nx, 0)
                            sp.wait_ge(score_full, score_index(b, g, score_item(1, 1, PROBS_U[1])))
                            copy_keys()
                        sp.wait_ge(pv_done, prob_index(b, g, p, 0, PROBS_P) + P_RING)
                        sp.dma_start(v_g[p][:], v_all[:, :, bass.ds(nx * D, D)]).then_inc(v_in[p], 16)
                copy_queries(b, HKV - 1, 1)
                sp.wait_ge(mid_done, 2 * b + 2)
                if not last:
                    sp.dma_start(x_in[:], one(x_v, b + 1)).then_inc(x_loaded, 16)
                sp.wait_ge(out_ready, 2 * b + 2)
                sp.dma_start(one(out_v, b), x_mid[:]).then_inc(out_stored, 16)

            def one(v, b):
                return v[bass.ds(b, 1), :, :, :].rearrange("o p n d -> (o p) n d")

            with sp.Fori(0, B - 1) as b:
                batch(b, False)
            batch(B - 1, True)
            sp.wait_ge(out_stored, 16 * B + 16)

        @block.tensor
        def _(pe):
            mm = nc.tensor.matmul
            pe.sem_inc(pv_done, P_RING)
            pe.sem_inc(sum_done, 2)

            def split_product(dst, w, x, done=None):
                mm(dst, w[0], x[0], start=True, stop=False)
                mm(dst, w[1], x[0], start=False, stop=False)
                ins = mm(dst, w[0], x[1], start=False, stop=True)
                if done is not None:
                    ins.then_inc(done, 1)

            def project(b, g, k):
                n, c = k // 2, k % 2
                i = project_index(b, g, k)
                if k in (0, PROJ_A):
                    pe.wait_ge(slab_a_in if k == 0 else slab_b_in, 16 * (b * HKV + g + 1))
                pe.wait_ge(score_read, i + 1)
                w = [slab_a[:, a, n * 128:n * 128 + 128] if k < PROJ_A else slab_b[:, a, :] for a in range(2)]
                x = [xT[:, a, c * HALF:c * HALF + HALF] for a in range(2)]
                split_product(score[i_bank(g, k)][:, :], w, x, score_full)

            def block_scores(b, g, p, c, n):
                h, i, kh, width = pieces(c)[n]
                q = prob_index(b, g, p, c, n)
                if n == 0:
                    pe.wait_ge(rope_low, rope_index(b, g, (PROJ_A if p == 0 else ROPES_G) - 1 + c) + 2)
                    if p == 1 and c == 0:
                        pe.wait_ge(k_copied, 48 * (b * HKV + g + 2))
                pe.wait_ge(max_read, q + 1)
                dst, whole = block_max[(c * PROBS_U[0] + n) % M_RING], 256 if width <= 256 else HALF
                diagonal = kh == c
                ins = mm(dst[:, 0:whole], qa[p][h][:, i * 128:i * 128 + 128], kk[p][:, kh * HALF:kh * HALF + whole],
                         start=True, stop=not diagonal)
                if diagonal:
                    ins = mm(dst[:, width - 128:width], identb, tri_q, start=False, stop=True)
                ins.then_inc(max_full, 1)

            def max_rows(b, g, p, c, last=False):
                i = row_index(b, g, p, c, last)
                bank = score[bank_of(row_item(p, c, last))]
                pe.wait_ge(max_ready, unit_index(b, g, p, c) + 1)
                pe.wait_ge(score_read, i + 1)
                for h in range(2):
                    r = 64 * (1 - h)
                    for t in range(4):
                        ins = mm(bank[r:r + 2, t * 128:t * 128 + 128], neg_max[:, c, h, t, :], identb,
                                 start=True, stop=True)
                ins.then_inc(score_full, 1)

            def sums(b, g, p, c):
                v = unit_index(b, g, p, c)
                pe.wait_ge(p_added, prob_index(b, g, p, c, PROBS_U[c]) + P_RING)
                pe.wait_ge(sum_read, v + 1)
                for h in range(2):
                    ins = mm(m_bank[64 * h:64 * h + 64, :], ones, psums[:, c, h, :], start=True, stop=True)
                ins.then_inc(sum_done, 1)

            def scores(b, g, p, c, j, last):
                off = max(0, j - 4 * c) * 128
                even = off // 256 * 256
                for h in range(2):
                    item = score_item(p, c, 2 * j + h, last)
                    if j == 0 and h == 0:
                        pe.wait_ge(score_read, row_index(b, g, p, c, last) + 1 + E_RING)
                        if c == 0:
                            pe.wait_ge(q_copied, 80 * (b * HKV + g) + 48 + 32 * p)
                    pe.wait_ge(score_read, score_index(b, g, item) + 1)
                    dst = score[bank_of(item)]
                    cols = slice(c * HALF + even, c * HALF + HALF)
                    mm(dst[:, even:], kk[p][:, j * 128:j * 128 + 128], qa[p][h][:, cols], start=True, stop=False)
                    ins = mm(dst[:, even:], kl[p][h][:, j * 128:j * 128 + 128], qb[p][h][:, cols],
                             start=False, stop=j < 4 * c)
                    if j >= 4 * c:
                        ins = mm(dst[:, off:off + 128], identb, tri_k, start=False, stop=True)
                    ins.then_inc(score_full, 1)

            def outputs(b, g, p, c, t, last):
                off = max(0, t - 4 * c) * 128
                if t == 0:
                    pe.wait_ge(o_kept, unit_index(b, g, p, c) + 1)
                    if c == 0:
                        pe.wait_ge(v_in[p], 16 * (b * HKV + g + 1))
                for h in range(2):
                    k = c * PROBS_U[0] + 2 * t + h
                    item = score_item(p, c, 2 * t + h, last)
                    pe.wait_ge(score_read, score_index(b, g, item) + 1 + E_RING)
                    mm(o_bank[c][64 * h:64 * h + 64, off:], v_g[p][:, t, :], probs[:, k % P_RING, off:],
                       start=(t == 0), stop=(t == 4 * c + 3)).then_inc(pv_done, 1)

            def unit(b, g, p, c, last):
                steps = 4 * (c + 1)
                for j in range(steps):
                    scores(b, g, p, c, j, last)
                    for piece in piece_plan(p, c, j, b, g, last):
                        block_scores(*piece)
                    if j == SUM_STEP:
                        for unit_before in before(g, p, c):
                            sums(b, *unit_before)
                    if j == steps - 1:
                        if c == 0:
                            max_rows(b, g, p, 1, last)
                        elif p == 0:
                            max_rows(b, g, 1, 0, last)
                        elif not last:
                            max_rows(b, g + 1, 0, 0)
                    if j >= LAG:
                        outputs(b, g, p, c, j - LAG, last)
                    else:
                        for g0, p0, c0 in before(g, p, c):
                            outputs(b, g0, p0, c0, 4 * c0 + 4 - LAG + j, last)
                for k in project_plan(p, c, last):
                    project(b, g + 1, k)

            pe.wait_ge(consts_in, 32)
            pe.wait_ge(cb_ready, 1)
            pe.wait_ge(zeroed, 2)
            with pe.Fori(0, B) as b:
                for t in range(TILES):
                    pe.wait_ge(ln_done, TILES * b + t + 1)
                    ins = nc.tensor.transpose(block_max[t // 4][:, t % 4 * 128:t % 4 * 128 + 128], x_norm[:, t, :], ident)
                    if t % 4 == 3:
                        ins.then_inc(x_turned, 1)
                pe.wait_ge(x_split, 2 * b + 2)
                for k in range(ROPES_G):
                    project(b, 0, k)
                for t in range(TILES):
                    u = t // 2
                    if t % 2 == 0 and u >= 2:
                        pe.wait_ge(v_kept, 4 * b + u - 1)
                    split_product(o_bank[u % 2][:, t % 2 * 256:t % 2 * 256 + 256],
                                  [xT[:, a, t * 128:t * 128 + 128] for a in range(2)], [w_v[:, a, :] for a in range(2)],
                                  v_proj if t % 2 else None)
                pe.wait_ge(v_kept, 4 * b + 4)
                for n in range(PROBS_U[0]):
                    block_scores(b, 0, 0, 0, n)
                for n in range(EARLY):
                    block_scores(b, 0, 0, 1, n)
                max_rows(b, 0, 0, 0)
                units(pe, lambda *at: unit(b, *at))
                for t in range(8 - LAG, 8):
                    outputs(b, HKV - 1, 1, 1, t, True)
                sums(b, HKV - 1, 1, 1)

                pe.wait_ge(ffn_w_in, 16 * FFN_LOADS)
                pe.wait_ge(o_kept, UNITS * b + UNITS + 2)
                for t in range(TILES):
                    for s in range(NP):
                        ins = mm(o_bank[t // 4][:, t % 4 * 128:t % 4 * 128 + 128], attnT[:, s, t * 128:t * 128 + 128],
                                 w_o[:, s, :], start=(s == 0), stop=(s == NP - 1))
                    if t % 4 == 3:
                        ins.then_inc(wo_done, 1)
                for t in range(TILES):
                    if t == 0:
                        pe.wait_ge(mid_done, 2 * b + 2)
                    ins = nc.tensor.transpose(block_max[t // 4][:, t % 4 * 128:t % 4 * 128 + 128], x_norm[:, t, :], ident)
                    if t % 4 == 3:
                        ins.then_inc(x2_turned, 1)

                for c in range(2):
                    pe.wait_ge(x2_kept, 2 * b + c + 1)
                    mm(score[c][:, :], w_lin0[:], x2T[:, c, :], start=True, stop=True).then_inc(lin0_done, 1)
                for c in range(2):
                    pe.wait_ge(h_kept, 2 * b + c + 1)
                    if c == 0:
                        pe.wait_ge(x2_kept, 2 * b + 2)
                    mm(score[c][:, :], w_swi[:, 0, :], hT[:, c, :], start=True, stop=True)
                    mm(block_max[c][:, :], w_swi[:, 1, :], hT[:, c, :], start=True, stop=True).then_inc(swi1_done, 1)
                for c in range(2):
                    pe.wait_ge(h1_kept, 2 * b + c + 1)
                    for t in range(4):
                        ins = mm(gate_bank[c][:, t * NE:t * NE + NE], h1T[:, c, t * 128:t * 128 + 128], gate_wT[:],
                                 start=True, stop=True)
                    ins.then_inc(gate_done, 1)
                for i in range(NI + 2):
                    if i == CB_FIRST - 1:
                        for c in range(2):
                            pe.wait_ge(gate_parts, 2 * b + c + 1)
                            for t in range(4):
                                ins = nc.tensor.transpose(gate_bank[c][:, :].bitcast(BF16)[:, t * 128:t * 128 + 128],
                                                          gpart[:, c, t, :], identb)
                            ins.then_inc(gate_turned, 1)
                    if i < NI:
                        k, c = items[i]
                        if i >= 2:
                            pe.wait_ge(ex_g, NI * b + i - 1)
                            pe.wait_ge(ex_gu, NI * b + i - 1)
                        mm(score[c][:, :], w_exp[:, 0, k, :], h1T[:, c, :], start=True, stop=True)
                        ins = mm(block_max[c][:, :], w_exp[:, 1, k, :], h1T[:, c, :], start=True, stop=True)
                        if k < NE:
                            r = i - CB_FIRST
                            pe.wait_ge(comb_kept, 2 * b + c + 1)
                            if r >= 2:
                                pe.wait_ge(ex_guc, (NI - CB_FIRST) * b + r - 1)
                            ins = mm(gate_bank[c][:, :], cb[:, C_SEL + k * 128:C_SEL + k * 128 + 128], combT[:, c, :],
                                     start=True, stop=True)
                        ins.then_inc(ex_full, 1)
                    if i >= 2:
                        k, c = items[i - 2]
                        if k < NE:
                            pe.wait_ge(ex_guc, (NI - CB_FIRST) * b + i - 2 - CB_FIRST + 1)
                        else:
                            pe.wait_ge(ex_gu, NI * b + i - 1)
                        mm(o_bank[c][:, :], w_exp[:, 2, k, :], (gucT if k < NE else guT)[:, c, :],
                           start=(i - 2 < 2), stop=(i - 2 >= NI - 2)).then_inc(ex_y, 1)
                for c in range(2):
                    pe.wait_ge(y_kept, 2 * b + c + 1)
                    mm(score[c][:, :], w_lin1[:], yT[:, c, :], start=True, stop=True).then_inc(lin1_done, 1)
                for c in range(2):
                    pe.wait_ge(h3_kept, 2 * b + c + 1)
                    mm(score[c][:, :], w_swi[:, 2, :], hT[:, c, :], start=True, stop=True)
                    mm(block_max[c][:, :], w_swi[:, 3, :], hT[:, c, :], start=True, stop=True).then_inc(swi2_done, 1)
                for c in range(2):
                    pe.wait_ge(hf_kept, 2 * b + c + 1)
                    for t in range(4):
                        ins = nc.tensor.transpose(gate_bank[c][:, t * 128:t * 128 + 128],
                                                  h1T[:, c, t * 128:t * 128 + 128], ident)
                    ins.then_inc(hf_turned, 1)

        @block.scalar
        def _(act):
            A = nc.scalar.activation
            act.sem_inc(score_read, E_RING)

            def keep_raw(b, g, k):
                i, r = project_index(b, g, k), rope_index(b, g, k)
                before = 2 if k < 2 else 6 if k < PROJ_A else 4
                act.wait_ge(score_full, i + 1)
                act.wait_ge(swapped, r - before + 1 + ROPES_G)
                A(raw[:, k % 4, :], score[i_bank(g, k)][:, :], ACT.Copy).then_inc(score_read, 1)

            def keep_high(b, g, k):
                r, c = rope_index(b, g, k), k % 2
                cols = slice(c * HALF, c * HALF + HALF)
                act.wait_ge(rope_sum, r + 1)
                if k < 2:
                    act.wait_ge(k_copied, 48 * (b * HKV + g + 1))
                    A(kk[0][:, cols], roped[:, c, :], ACT.Copy).then_inc(rope_high, 1)
                    return
                p = 0 if k < PROJ_A else 1
                for h in range(2):
                    ins = A(qa[p][h][64 * h:64 * h + 64, cols], roped[64 * h:64 * h + 64, c, :], ACT.Copy)
                ins.then_inc(rope_high, 1)

            def keep_max(b, g, p, c, last=False):
                cols = slice(c * HALF, c * HALF + HALF)
                bank = score[bank_of(row_item(p, c, last))]
                act.wait_ge(score_full, row_index(b, g, p, c, last) + 1)
                A(qb[p][0][64:66, cols], bank[64:66, :], ACT.Copy)
                A(qb[p][1][0:2, cols], bank[0:2, :], ACT.Copy).then_inc(score_read, 1)

            def reciprocals(b, g, p, c):
                v = unit_index(b, g, p, c)
                act.wait_ge(sum_done, v + 1 + 2)
                act.wait_ge(o_kept, v + 2)
                A(recip[:], m_bank[:, :], ACT.Ln).then_inc(log_done, 1)
                act.wait_ge(log_done, v + 1)
                A(recip[:], recip[:], ACT.Exp, scale=-1.0).then_inc(recip_ready, 1)

            def deviations(b, n, first, count):
                act.wait_ge(var_ready, NORMS * b + n + 1)
                A(dev[:, first:first + count], mean_var[:, first:first + count, 1], ACT.Sqrt,
                  bias=cf[:, C_EPS:C_EPS + 1]).then_inc(dev_ready, 1)

            def unit(b, g, p, c, last):
                steps = 4 * (c + 1)
                for j in range(steps):
                    for stage, ahead, k in rope_plan(p, c, j, last):
                        if stage == "low":
                            keep_high(b, g + ahead, k)
                    off = max(0, j - 4 * c) * 128
                    for h in range(2):
                        k = c * PROBS_U[0] + 2 * j + h
                        item = score_item(p, c, 2 * j + h, last)
                        m = prob_index(b, g, p, 0, k)
                        act.wait_ge(score_full, score_index(b, g, item) + 1)
                        act.wait_ge(pv_done, m + 1)
                        act.wait_ge(p_added, m + 1)
                        A(probs[:, k % P_RING, off:], score[bank_of(item)][:, off:], ACT.Exp,
                          scale=float(D) ** -0.5).then_inc(score_read, 1)
                    if j == RECIP_STEP:
                        for unit_before in before(g, p, c):
                            reciprocals(b, *unit_before)
                if c == 0:
                    keep_max(b, g, p, 1, last)
                elif p == 0:
                    keep_max(b, g, 1, 0, last)
                elif not last:
                    keep_max(b, g + 1, 0, 0)
                for k in project_plan(p, c, last):
                    keep_raw(b, g + 1, k)

            act.wait_ge(consts_in, 32)
            A(cb[:], cb_raw, ACT.Copy).then_inc(cb_ready, 1)
            act.wait_ge(w_in, 64)
            wr = w_raw[:, 0:HKV * 384].rearrange("p (g n) -> p g n", g=HKV)
            A(w_qk[:, 0, :, :], wr, ACT.Copy)
            A(w_v[:, 0, :], w_raw[:, HKV * 384:HKV * 384 + 256], ACT.Copy).then_inc(w_high, 1)

            act.wait_ge(consts_in, 32)
            with act.Fori(0, B) as b:
                deviations(b, 0, 0, TILES)
                for a in range(2):
                    act.wait_ge(x_turned, 2 * b + a + 1)
                    A(xT[:, 0, a * HALF:a * HALF + HALF], block_max[a][:, :], ACT.Copy).then_inc(x_high, 1)
                for k in range(ROPES_G):
                    if k == PROJ_A:
                        for kh in range(2):
                            keep_high(b, 0, kh)
                    keep_raw(b, 0, k)
                for u in range(4):
                    act.wait_ge(v_proj, 4 * b + u + 1)
                    A(v_all[:, 2 * u:2 * u + 2, :], o_bank[u % 2][:, :].rearrange("p (t n) -> p t n", t=2),
                      ACT.Copy).then_inc(v_kept, 1)
                for k in range(2, PROJ_A):
                    keep_high(b, 0, k)
                keep_max(b, 0, 0, 0)
                nc.scalar.preload_act_table_set("natural_log_exp_and_others")
                units(act, lambda *at: unit(b, *at))
                reciprocals(b, HKV - 1, 1, 1)

                act.wait_ge(ffn_w_in, 16 * FFN_LOADS)
                for a in range(2):
                    deviations(b, 1 + a, 4 * a, 4)
                deviations(b, 3, 0, TILES)
                for c in range(2):
                    act.wait_ge(x2_turned, 2 * b + c + 1)
                    A(x2T[:, c, :], block_max[c][:, :], ACT.Copy).then_inc(x2_kept, 1)
                for c in range(2):
                    act.wait_ge(lin0_done, 2 * b + c + 1)
                    A(hT[:, c, :], score[c][:, :], ACT.Identity, bias=biases[:, 0:1]).then_inc(h_kept, 1)
                for c in range(2):
                    act.wait_ge(swi1_done, 2 * b + c + 1)
                    A(aT[:, c, :], score[c][:, :], ACT.Silu, bias=biases[:, 1:2]).then_inc(a_kept, 1)
                for c in range(2):
                    act.wait_ge(gate_z, 2 * b + c + 1)
                    A(gex[:, c, :, :], gz[:, c, :, :], ACT.Exp).then_inc(gate_exp, 1)
                for i in range(NI):
                    c = items[i][1]
                    if i == CB_FIRST:
                        for cc in range(2):
                            act.wait_ge(gate_turned, 2 * b + cc + 1)
                            A(combT[:, cc, :], gate_bank[cc][:, :].bitcast(BF16)[:, 0:HALF], ACT.Copy).then_inc(comb_kept, 1)
                    act.wait_ge(ex_full, NI * b + i + 1)
                    if i >= 2:
                        act.wait_ge(ex_gu, NI * b + i - 1)
                    A(gT[:, c, :], score[c][:, :], ACT.Silu).then_inc(ex_g, 1)
                for c in range(2):
                    act.wait_ge(ex_y, NI * b + NI - 1 + c)
                    A(yT[:, c, :], o_bank[c][:, :], ACT.Copy).then_inc(y_kept, 1)
                for c in range(2):
                    act.wait_ge(lin1_done, 2 * b + c + 1)
                    A(hT[:, c, :], score[c][:, :], ACT.Identity, bias=biases[:, 3:4]).then_inc(h3_kept, 1)
                for c in range(2):
                    act.wait_ge(swi2_done, 2 * b + c + 1)
                    A(aT[:, c, :], score[c][:, :], ACT.Silu, bias=biases[:, 4:5]).then_inc(a2_kept, 1)
                for c in range(2):
                    deviations(b, 4 + c, 4 * c, 4)

        @block.gpsimd
        def _(pool):
            pool.sem_inc(p_added, P_RING)
            for p in range(2):
                for h in range(2):
                    r = 64 * (1 - h)
                    pool.memset(kl[p][h][:].bitcast(F32), 0.0)
                    ins = pool.memset(qb[p][h][:].bitcast(F32), 0.0)
            ins.then_inc(zeroed, 1)
            pool.wait_ge(zeroed, 1)
            for p in range(2):
                for h in range(2):
                    r = 64 * (1 - h)
                    ins = pool.memset(kl[p][h][r:r + 2, :].bitcast(F32), 1.0)
            ins.then_inc(zeroed, 1)
            pool.wait_ge(consts_in, 32)

            def add(b, g, p, c, j, last):
                if j == 0:
                    return
                off = max(0, j - 4 * c) * 128
                for h in range(2):
                    k = c * PROBS_U[0] + 2 * j + h
                    m = prob_index(b, g, p, 0, k)
                    dst = psums[:, c, h, off:]
                    item = score_item(p, c, 2 * j + h, last)
                    pool.wait_ge(score_read, score_index(b, g, item) + 1 + E_RING)
                    if j == 1:
                        if h == 0:
                            pool.wait_ge(sum_done, unit_index(b, g, p, c) + 1)
                        ins = pool.tensor_tensor(dst, probs[:, (k - 2) % P_RING, off:], probs[:, k % P_RING, off:],
                                                 ALU.add)
                        if off:
                            ins = pool.tensor_copy(psums[:, c, h, 0:off], probs[:, (k - 2) % P_RING, 0:off])
                        ins.then_inc(p_added, 3 if h else 1)
                    else:
                        pool.wait_ge(p_added, m - 1 + P_RING)
                        pool.tensor_tensor(dst, dst, probs[:, k % P_RING, off:], ALU.add).then_inc(p_added, 1)

            def unit(b, g, p, c, last):
                for j in range(4 * (c + 1)):
                    add(b, g, p, c, j, last)
            with pool.Fori(0, B) as b:
                units(pool, lambda *at: unit(b, *at))

        @block.vector
        def _(dve):
            V = nc.vector
            dve.sem_inc(max_read, M_RING)
            dve.sem_inc(sum_read, 1)
            dve.sem_inc(o_kept, 2)
            dve.sem_inc(swapped, ROPES_G)
            dve.sem_inc(rope_low, 2)

            class Steps:
                def __init__(self, b):
                    self.b, self.base, self.n, self.deviations = b, b * STEPS_B, 0, 0

                def __call__(self, ins):
                    self.n += 1
                    ins.then_inc(ln_step, 1)
                    dve.wait_ge(ln_step, self.base + self.n)

            def statistics(step, src, tiles):
                n = len(tiles)
                for t in tiles:
                    ins = V.bn_stats(stats[:, t, :], src(t))
                step(ins)
                V.memset(unused[:], 0.0)
                for t in tiles:
                    ins = V.bn_aggr(mean_var[:, t, :], stats[:, t, :])
                step.deviations += 1
                ins.then_inc(var_ready, 1)
                dve.wait_ge(dev_ready, NORMS * step.b + step.deviations)
                step(V.reciprocal(rstd[:, tiles[0]:tiles[0] + n], dev[:, tiles[0]:tiles[0] + n]))

            def normalise(dst, src, t):
                return V.tensor_scalar(dst, src, mean_var[:, t, 0:1], rstd[:, t:t + 1], ALU.subtract, ALU.mult)

            def rope_work(b, g, stage, k):
                r, c = rope_index(b, g, k), k % 2
                cols = slice(c * HALF, c * HALF + HALF)
                if stage == "turn":
                    dve.wait_ge(rope_low, r + 1)
                    dve.wait_ge(score_read, project_index(b, g, k) + 1 + E_RING)
                    V.tensor_tensor(roped[:, c, :], raw[:, k % 4, :], cf[:, C_COS + c * HALF:C_COS + c * HALF + HALF],
                                    ALU.mult)
                    V.stream_shuffle(turned[:, c, :], raw[:, k % 4, :], SWAP).then_inc(swapped, 1)
                elif stage == "sum":
                    dve.wait_ge(swapped, r + 1 + ROPES_G)
                    V.tensor_tensor(turned[:, c, :], turned[:, c, :], cf[:, C_SIN + c * HALF:C_SIN + c * HALF + HALF],
                                    ALU.mult).then_inc(sin_done, 1)
                    dve.wait_ge(sin_done, r + 1)
                    V.tensor_tensor(roped[:, c, :], roped[:, c, :], turned[:, c, :], ALU.add).then_inc(rope_sum, 1)
                else:
                    dve.wait_ge(rope_high, r + 1)
                    if k < 2:
                        ins = V.tensor_tensor(kl[0][0][0:64, cols], roped[0:64, c, :], kk[0][0:64, cols], ALU.subtract)
                    p = 0 if k < PROJ_A else 1
                    for h in range(2) if k >= 2 else ():
                        half = slice(64 * h, 64 * h + 64)
                        ins = V.tensor_tensor(qa[p][h][64 * (1 - h):64 * (1 - h) + 64, cols], roped[half, c, :],
                                              qa[p][h][half, cols], ALU.subtract)
                    ins.then_inc(rope_low, 1)

            def block_maximum(b, g, p, c, n):
                h, i, kh, width = pieces(c)[n]
                q = prob_index(b, g, p, c, n)
                dve.wait_ge(max_full, q + 1)
                V.reduce_max(maxes[:, c, h, kh, i % 4:i % 4 + 1], block_max[(c * PROBS_U[0] + n) % M_RING][:, 0:width], AX_X
                             ).then_inc(max_read, 1)
                if n == PROBS_U[c] - 1:
                    negate(b, g, p, c)

            def negate(b, g, p, c):
                v = unit_index(b, g, p, c)
                m0 = (b * NP + g * 2 + p) * 3 + c
                dve.wait_ge(max_read, prob_index(b, g, p, c, PROBS_U[c]) + M_RING)
                top_v = maxes[:, 0, :, 0, :]
                if c:
                    V.tensor_tensor(top[:], maxes[:, 1, :, 0, :], maxes[:, 1, :, 1, :], ALU.max).then_inc(max_step, 1)
                    dve.wait_ge(max_step, m0 + 1)
                    top_v, m0 = top[:], m0 + 1
                V.tensor_scalar(neg_max[:, c, :, :, 0], top_v, -1.0, None, ALU.mult).then_inc(max_step, 1)
                dve.wait_ge(max_step, m0 + 1)
                V.scalar_tensor_tensor(out=neg_max[:, c, :, :, 1], in0=top_v, scalar=-1.0, in1=neg_max[:, c, :, :, 0],
                                       op0=ALU.mult, op1=ALU.subtract).then_inc(max_ready, 1)

            def divide(b, g, p, c):
                v = unit_index(b, g, p, c)
                if isinstance(g, int):
                    dst = attnT[:, 2 * g + p, c * HALF:c * HALF + HALF]
                else:
                    dst = attnT[:, bass.ds(2 * g + p, 1), c * HALF:c * HALF + HALF].rearrange("p o t -> p (o t)")
                dve.wait_ge(recip_ready, v + 1)
                dve.wait_ge(pv_done, prob_index(b, g, p, c, PROBS_U[c]) + P_RING)
                V.scalar_tensor_tensor(out=dst, in0=o_bank[c][:, :], scalar=-1.0, in1=recip[:],
                                       op0=ALU.mult, op1=ALU.mult).then_inc(divide_step, 1)
                dve.wait_ge(divide_step, v + 1)
                V.tensor_tensor(recip[:], m_bank[:, :], recip[:], ALU.mult).then_inc(sum_read, 1)
                dve.wait_ge(sum_read, v + 2)
                V.scalar_tensor_tensor(out=dst, in0=recip[:], scalar=2.0, in1=dst,
                                       op0=ALU.subtract, op1=ALU.mult).then_inc(o_kept, 1)

            def unit(b, g, p, c, last):
                for j in range(4 * (c + 1)):
                    for piece in piece_plan(p, c, j, b, g, last):
                        block_maximum(*piece)
                    for stage, ahead, k in rope_plan(p, c, j, last):
                        rope_work(b, g + ahead, stage, k)
                    if j == DIVIDE_STEP[c]:
                        for unit_before in before(g, p, c):
                            divide(b, *unit_before)

            def route(step, b, c):
                ex = gex[:, c, :, :]
                mine = ex.unsqueeze(3).to_broadcast([128, 4, NE, NE])
                other = ex.unsqueeze(2).to_broadcast([128, 4, NE, NE])
                tie = cf[:, C_TIE:C_TIE + 64].rearrange("p (a e j) -> p a e j", a=1, e=NE).to_broadcast([128, 4, NE, NE])
                if c:
                    dve.wait_ge(gate_parts, 2 * b + 1)
                dve.wait_ge(gate_exp, 2 * b + c + 1)
                V.tensor_tensor(gcmp, other, mine, ALU.is_gt)
                step(V.tensor_tensor(geq, other, mine, ALU.is_equal))
                step(V.tensor_tensor(geq, geq, tie, ALU.mult))
                step(V.tensor_tensor(gcmp, gcmp, geq, ALU.add))
                step(V.tensor_reduce(grank[:], gcmp, AX_X, ALU.add))
                step(V.scalar_tensor_tensor(out=grank[:], in0=grank[:], scalar=TOPK - 0.5, in1=ex,
                                            op0=ALU.is_lt, op1=ALU.mult))
                step(V.tensor_reduce(gsum[:], grank[:], AX_X, ALU.add))
                step(V.reciprocal(gsum[:], gsum[:]))
                step(V.tensor_tensor(grank[:], grank[:], gsum[:].unsqueeze(2).to_broadcast([128, 4, NE]), ALU.mult))
                for part in range(3):
                    cols = slice(part * NE, part * NE + NE)
                    ins = V.tensor_copy(gpart[:, c, :, cols], grank[:])
                    if part < 2:
                        step(ins)
                        step(V.tensor_tensor(grank[:], grank[:], gpart[:, c, :, cols], ALU.subtract))
                ins.then_inc(gate_parts, 1)

            dve.wait_ge(w_high, 1)
            wr = w_raw[:, 0:HKV * 384].rearrange("p (g n) -> p g n", g=HKV)
            V.tensor_tensor(w_qk[:, 1, :, :], wr, w_qk[:, 0, :, :], ALU.subtract)
            V.tensor_tensor(w_v[:, 1, :], w_raw[:, HKV * 384:HKV * 384 + 256], w_v[:, 0, :], ALU.subtract).then_inc(w_split, 1)
            dve.wait_ge(zeroed, 2)
            dve.wait_ge(consts_in, 32)

            with dve.Fori(0, B) as b:
                step = Steps(b)
                dve.wait_ge(x_loaded, 16 * (b + 1))
                statistics(step, lambda t: x_in[:, t, :], list(range(TILES)))
                for t in range(TILES):
                    normalise(x_norm[:, t, :], x_in[:, t, :], t).then_inc(ln_done, 1)
                for a in range(2):
                    cols = slice(a * HALF, a * HALF + HALF)
                    dve.wait_ge(x_high, 2 * b + a + 1)
                    V.tensor_tensor(xT[:, 1, cols], block_max[a][:, :], xT[:, 0, cols], ALU.subtract).then_inc(x_split, 1)
                for two in ((0, 1), (2, 3)):
                    for stage in ("turn", "sum", "low"):
                        for k in two:
                            rope_work(b, 0, stage, k)
                for n in range(PROBS_U[0]):
                    block_maximum(b, 0, 0, 0, n)
                for n in range(EARLY):
                    block_maximum(b, 0, 0, 1, n)
                for stage in ("turn", "sum"):
                    for k in range(PROJ_A, ROPES_G):
                        rope_work(b, 0, stage, k)
                units(dve, lambda *at: unit(b, *at))
                divide(b, HKV - 1, 1, 1)

                dve.wait_ge(out_stored, 16 * b + 16)
                for a in range(2):
                    tiles = list(range(4 * a, 4 * a + 4))
                    dve.wait_ge(wo_done, 2 * b + a + 1)
                    src = lambda t: o_bank[t // 4][:, t % 4 * 128:t % 4 * 128 + 128]
                    statistics(step, src, tiles)
                    for t in tiles:
                        ins = normalise(x_mid[:, t, :], src(t), t)
                    step(ins)
                    V.tensor_tensor(x_mid[:, 4 * a:4 * a + 4, :], x_mid[:, 4 * a:4 * a + 4, :], x_in[:, 4 * a:4 * a + 4, :],
                                    ALU.add).then_inc(mid_step, 1)
                dve.wait_ge(mid_step, 2 * b + 2)
                statistics(step, lambda t: x_mid[:, t, :], list(range(TILES)))
                for t in range(TILES):
                    ins = normalise(x_norm[:, t, :], x_mid[:, t, :], t)
                ins.then_inc(mid_done, 2)

                for c in range(2):
                    dve.wait_ge(a_kept, 2 * b + c + 1)
                    V.scalar_tensor_tensor(out=h1T[:, c, :], in0=block_max[c][:, :], scalar=biases[:, 2:3], in1=aT[:, c, :],
                                           op0=ALU.add, op1=ALU.mult).then_inc(h1_kept, 1)
                for c in range(2):
                    if c:
                        dve.wait_ge(gate_z, 2 * b + 1)
                    dve.wait_ge(gate_done, 2 * b + c + 1)
                    lg = gate_bank[c][:, 0:4 * NE].rearrange("p (t e) -> p t e", e=NE)
                    step(V.tensor_reduce(gsum[:], lg, AX_X, ALU.max))
                    V.tensor_tensor(gz[:, c, :, :], lg, gsum[:].unsqueeze(2).to_broadcast([128, 4, NE]),
                                    ALU.subtract).then_inc(gate_z, 1)
                step(V.memset(psums[:, 0, 0, :], 0.0))
                for i in range(NI):
                    k, c = items[i]
                    if i == 2:
                        route(step, b, 0)
                        route(step, b, 1)
                    dve.wait_ge(ex_g, NI * b + i + 1)
                    if i >= 2:
                        dve.wait_ge(ex_y, NI * b + i - 1)
                    V.tensor_tensor(guT[:, c, :], block_max[c][:, :], gT[:, c, :], ALU.mult).then_inc(ex_gu, 1)
                    if k < NE:
                        dve.wait_ge(ex_gu, NI * b + i + 1)
                        V.tensor_tensor(gucT[:, c, :], gate_bank[c][:, :], guT[:, c, :], ALU.mult).then_inc(ex_guc, 1)
                for c in range(2):
                    dve.wait_ge(a2_kept, 2 * b + c + 1)
                    V.scalar_tensor_tensor(out=h1T[:, c, :], in0=block_max[c][:, :], scalar=biases[:, 5:6], in1=aT[:, c, :],
                                           op0=ALU.add, op1=ALU.mult).then_inc(hf_kept, 1)
                for c in range(2):
                    tiles = list(range(4 * c, 4 * c + 4))
                    dve.wait_ge(hf_turned, 2 * b + c + 1)
                    src = lambda t: gate_bank[t // 4][:, t % 4 * 128:t % 4 * 128 + 128]
                    statistics(step, src, tiles)
                    for t in tiles:
                        ins = normalise(x_norm[:, t, :], src(t), t)
                    step(ins)
                    V.tensor_tensor(x_mid[:, 4 * c:4 * c + 4, :], x_mid[:, 4 * c:4 * c + 4, :],
                                    x_norm[:, 4 * c:4 * c + 4, :], ALU.add).then_inc(out_ready, 1)
                assert step.n == STEPS_B, step.n


def constants():
    cf = np.zeros((128, C_F32), np.float32)
    cf[:, C_ID:C_ID + 128] = np.eye(128)
    cf[:, C_EPS] = EPS
    cf[:, C_ONES:C_ONES + D] = 1.0
    cf[:, C_TIE:C_TIE + 64] = (np.arange(NE)[None, :] < np.arange(NE)[:, None]).reshape(1, 64)
    inv_freq = (np.float32(1.0) / np.float32(ROPE_THETA) ** (np.arange(0, D, 2, dtype=np.float32) / np.float32(D)))
    freqs = np.arange(S, dtype=np.float32)[:, None] * inv_freq.astype(np.float32)[None, :]
    emb = np.concatenate([freqs, freqs], axis=-1)[:, 0::2]
    pair = (np.arange(128) % D) // 2
    sign = np.where(np.arange(128) % 2 == 0, -1.0, 1.0).astype(np.float32)
    cf[:, C_COS:C_COS + S] = np.cos(emb).T[pair]
    cf[:, C_SIN:C_SIN + S] = np.sin(emb).T[pair] * sign[:, None]
    cb = np.zeros((128, C_BF), np.float32)
    cb[:, C_IDB:C_IDB + 128] = np.eye(128)
    at = np.arange(128)
    cb[:, C_TRIQ:C_TRIQ + 128] = np.where(at[None, :] > at[:, None], MASKED, 0.0)
    cb[:, C_TRIK:C_TRIK + 128] = np.where(at[:, None] > at[None, :], MASKED, 0.0)
    for e in range(NE):
        for part in range(3):
            cb[part * NE + e, C_SEL + e * 128:C_SEL + e * 128 + 128] = 1.0
    return cf, cb


_INS = {"x": "L0_attn_hidden_states", "wq": "L0_attn_Wq", "wk": "L0_attn_Wk", "wv": "L0_attn_Wv", "wo": "L0_attn_Wo"}
_INS.update({n: "L0_ffn_" + n for n in (
    "lin0_w", "lin0_b", "swi1_w1", "swi1_b1", "swi1_w2", "swi1_b2", "gate_w", "exp_w1", "exp_w3", "exp_w2",
    "sh_w1", "sh_w3", "sh_w2", "lin1_w", "lin1_b", "swi2_w1", "swi2_b1", "swi2_w2", "swi2_b2")})


def kernel(**inputs):
    import numpy as _np
    import concourse.bacc as _bacc
    from concourse import mybir as _mybir
    from concourse.bass_utils import run_bass_kernel_spmd as _run

    nc = _bacc.Bacc("TRN2", target_bir_lowering=False, num_devices=1)
    arrays = {n: _np.ascontiguousarray(inputs[name]) for n, name in _INS.items()}
    arrays["gate_wT"] = _np.ascontiguousarray(arrays.pop("gate_w").T)
    arrays["cf"], arrays["cb"] = constants()
    io = {n: nc.dram_tensor(f"in_{n}", a.shape, _mybir.dt.from_np(a.dtype), kind="ExternalInput").ap()
          for n, a in arrays.items()}
    out = nc.dram_tensor("out_0", (B, S, HID), F32, kind="ExternalOutput").ap()
    build(nc, io, out)
    r = _run(nc, [{f"in_{n}": a for n, a in arrays.items()}], core_ids=[0])
    return r.results[0]["out_0"]
```
